# Optimizing a Trainium2 kernel written in Bass

```python
import numpy as np
import jax
import jax.numpy as jnp

def _softmax(x, axis=-1):
    return jax.nn.softmax(x, axis=axis)
def _gelu(x):
    return jax.nn.gelu(x, approximate=True)
def _silu(x):
    return jax.nn.silu(x)
def _sigmoid(x):
    return jax.nn.sigmoid(x)
def _layernorm(x, axis=-1, eps=1e-5):
    m = jnp.mean(x, axis=axis, keepdims=True)
    v = jnp.var(x, axis=axis, keepdims=True)
    return (x - m) / jnp.sqrt(v + eps)
def _scatter_add(tgt, idx, src, axis=0):
    return tgt.at[idx].add(src)
def _segment_sum(src, seg, n):
    return jax.ops.segment_sum(src, seg, n)

kernel_name = 'mk_adj_preln_d4_adj_64_ae8ba7'

def setup_inputs(seed: int = 0):
    np.random.seed(seed)
    _w = jnp.asarray
    def _rec_inputs():
        import jax
        import jax.numpy as jnp
        _gk = jax.random.key(seed)
        x = -0.000929 + 1 * jax.random.normal(jax.random.fold_in(_gk, 1), (8192, 64), jnp.float32)
        _a = jax.random.bernoulli(jax.random.fold_in(_gk, 2), 0.00195312, (8192, 8192))
        _a = jnp.logical_or(_a, jnp.eye(8192, dtype=bool))
        _af = _a.astype(jnp.float32)
        _af = _af * jax.random.uniform(jax.random.fold_in(_gk, 3), (8192, 8192), jnp.float32, 0.05, 1)
        adj = _af
        return x, adj
    x, adj = _rec_inputs()
    def _L0_gnn_setup():
        import jax, jax.numpy as jnp
        import numpy as np
        HOP = 2
        N = 16384
        HIDDEN = 64
        key = jax.random.key(seed)
        k1, k2, k3 = jax.random.split(key, 3)
        user_embs = jax.random.normal(k1, (N, HIDDEN), dtype=jnp.float32)
        adj = jax.random.uniform(k2, (N, N), dtype=jnp.float32)
        limit = float(np.sqrt(6.0 / (2 * HIDDEN + HIDDEN)))
        W = jax.random.uniform(k3, (HOP, 2 * HIDDEN, HIDDEN), dtype=jnp.float32, minval=-limit, maxval=limit)
        return {'user_embs': user_embs, 'adj': adj, 'W': W}
    _L0_gnn_all = _L0_gnn_setup()
    _L0_gnn_in = {k: v for k, v in _L0_gnn_all.items() if k in ('W', )}
    del _L0_gnn_all

    def _L1_gnn_setup():
        import jax, jax.numpy as jnp
        import numpy as np
        N = 10000
        DIM = 64
        F_CONST = 1.0
        B_CONST = 0.1
        R_CONST = 0.01
        key = jax.random.key(seed)
        k1, k2 = jax.random.split(key)
        t = jnp.zeros((1,), dtype=jnp.float32)
        x = jax.random.uniform(k1, (N, DIM), dtype=jnp.float32)
        A = jax.random.uniform(k2, (N, N), dtype=jnp.float32)
        return {'t': t, 'x': x, 'A': A}
    _L1_gnn_all = _L1_gnn_setup()
    _L1_gnn_in = {k: v for k, v in _L1_gnn_all.items() if k in ('t', )}
    del _L1_gnn_all

    def _L2_gnn_setup():
        import jax, jax.numpy as jnp
        import numpy as np
        N = 8192
        DIN = 64
        DH = 64
        DOUT = 64
        SPARSITY = 0.01
        key = jax.random.key(seed)
        ks = jax.random.split(key, 9)
        x = jax.random.normal(ks[0], (N, DIN), dtype=jnp.float32)
        A = (jax.random.uniform(ks[1], (N, N)) < SPARSITY).astype(jnp.float32)
        left_weights = jax.random.normal(ks[2], (N, N), dtype=jnp.float32)

        def lin(k, fan_in, fan_out):
            k1, k2 = jax.random.split(k)
            bound = 1.0 / np.sqrt(fan_in)
            W = jax.random.uniform(k1, (fan_out, fan_in), minval=-bound, maxval=bound, dtype=jnp.float32)
            b = jax.random.uniform(k2, (fan_out,), minval=-bound, maxval=bound, dtype=jnp.float32)
            return (W, b)
        W0, b0 = lin(ks[3], DIN, DH)
        W1, b1 = lin(ks[4], DH, DH)
        W2, b2 = lin(ks[5], DH, DOUT)
        return {'x': x, 'A': A, 'left_weights': left_weights, 'W0': W0, 'b0': b0, 'W1': W1, 'b1': b1, 'W2': W2, 'b2': b2}
    _L2_gnn_all = _L2_gnn_setup()
    _L2_gnn_in = {k: v for k, v in _L2_gnn_all.items() if k in ('W0', 'b0', 'W1', 'b1', 'W2', 'b2', )}
    del _L2_gnn_all

    def _L3_gnn_setup():
        import jax, jax.numpy as jnp
        import numpy as np
        N = 16384
        IN_C = 64
        OUT_C = 64
        key = jax.random.key(seed)
        k1, k2, k3 = jax.random.split(key, 3)
        g_data = jax.random.normal(k1, (N, IN_C), dtype=jnp.float32)
        g_adj = jax.random.uniform(k2, (N, N), dtype=jnp.float32)
        bound = 1.44 * np.sqrt(6.0 / (IN_C + OUT_C))
        W = jax.random.uniform(k3, (IN_C, OUT_C), dtype=jnp.float32, minval=-bound, maxval=bound)
        return {'g_data': g_data, 'g_adj': g_adj, 'W': W}
    _L3_gnn_all = _L3_gnn_setup()
    _L3_gnn_in = {k: v for k, v in _L3_gnn_all.items() if k in ('W', )}
    del _L3_gnn_all

    return {
        "x": x,
        "adj": adj,
        "L0_gnn_W": _L0_gnn_in["W"],
        "L1_gnn_t": _L1_gnn_in["t"],
        "L2_gnn_W0": _L2_gnn_in["W0"],
        "L2_gnn_b0": _L2_gnn_in["b0"],
        "L2_gnn_W1": _L2_gnn_in["W1"],
        "L2_gnn_b1": _L2_gnn_in["b1"],
        "L2_gnn_W2": _L2_gnn_in["W2"],
        "L2_gnn_b2": _L2_gnn_in["b2"],
        "L3_gnn_W": _L3_gnn_in["W"],
    }

def reference(x, adj, L0_gnn_W, L1_gnn_t, L2_gnn_W0, L2_gnn_b0, L2_gnn_W1, L2_gnn_b1, L2_gnn_W2, L2_gnn_b2, L3_gnn_W):
    import jax
    import jax.numpy as jnp
    def _L0_gnn_ref(user_embs, adj, W):
        import jax, jax.numpy as jnp
        import numpy as np
        HOP = 2
        N = 16384
        HIDDEN = 64
        x = user_embs
        for k in range(HOP):
            agg = adj @ x
            x = jnp.tanh(jnp.concatenate([agg, x], axis=1) @ W[k])
        return x

    def _L1_gnn_ref(t, x, A):
        import jax, jax.numpy as jnp
        import numpy as np
        N = 10000
        DIM = 64
        F_CONST = 1.0
        B_CONST = 0.1
        R_CONST = 0.01
        Ax = A @ x
        outer = R_CONST * jnp.sum(x * Ax, axis=1, keepdims=True)
        return F_CONST - B_CONST * x - outer

    def _L2_gnn_ref(x, A, left_weights, W0, b0, W1, b1, W2, b2):
        import jax, jax.numpy as jnp
        import numpy as np
        N = 8192
        DIN = 64
        DH = 64
        DOUT = 64
        SPARSITY = 0.01
        w = left_weights * A
        for W, b in ((W0, b0), (W1, b1), (W2, b2)):
            x = w @ x
            x = x @ W.T + b
        return x

    def _L3_gnn_ref(g_data, g_adj, W):
        import jax, jax.numpy as jnp
        import numpy as np
        N = 16384
        IN_C = 64
        OUT_C = 64
        n = g_adj.shape[0]
        a = g_adj + jnp.eye(n, dtype=g_adj.dtype)
        deg = a.sum(axis=1)
        dinv = jnp.where(deg > 0, deg ** (-0.5), 0.0)
        a_norm = dinv[:, None] * a * dinv[None, :]
        out = a_norm @ g_data
        out = out @ W
        return out

    h = jnp.maximum(_layernorm(x, axis=-1), 0.0)
    x = x + _L0_gnn_ref(h, adj, L0_gnn_W)
    h = jnp.maximum(_layernorm(x, axis=-1), 0.0)
    x = x + _L1_gnn_ref(L1_gnn_t, h, adj)
    h = jnp.maximum(_layernorm(x, axis=-1), 0.0)
    x = x + _L2_gnn_ref(h, adj, adj, L2_gnn_W0, L2_gnn_b0, L2_gnn_W1, L2_gnn_b1, L2_gnn_W2, L2_gnn_b2)
    h = jnp.maximum(_layernorm(x, axis=-1), 0.0)
    x = x + _L3_gnn_ref(h, adj, L3_gnn_W)
    return x


_drawn_inputs = setup_inputs


def setup_inputs(seed=0):
    import zlib

    import numpy as np

    out = dict(_drawn_inputs(seed))
    spreads = {}
    factors = {'L2_gnn_b1': 4.743, 'L2_gnn_b2': 8.0}
    for name, (base, spread) in spreads.items():
        noise = np.random.default_rng([zlib.crc32(name.encode()), seed]).standard_normal(out[name].shape)
        drawn = base * np.exp(spread * noise) if base else spread * noise
        out[name] = jnp.asarray(drawn.astype(out[name].dtype))
    for name, factor in factors.items():
        out[name] = (out[name] * factor).astype(out[name].dtype)
    return out
```

```python
from contextlib import ExitStack

import concourse.bass as bass
from concourse import mybir

F32 = mybir.dt.float32
I32 = mybir.dt.int32
ALU = mybir.AluOpType
ACT = mybir.ActivationFunctionType
AX = mybir.AxisListType.X

P = 128
D = 64
SW = 1024
NT = SW // P
NQ = 4
BANK = 512
NI = SW // BANK
SWEEPS = 7
EPS = 1e-5
F_CONST, B_CONST, R_CONST = 1.0, 0.1, 0.01
TINY = 1.1754944e-38
RSQRT_GUESS = float(0x5F3759DF)
TURNED = (1, 2, 7)
BY_SQUARE = (4, 5, 6)


def graph_layers(nc, x, adj, wstack, wcat, bias, eye, out):
    NTILES = x.shape[1]
    T = NTILES // NT
    assert adj.shape[0] == T * T * NQ and T >= 2
    TRI = T * (T - 1) // 2
    FIRST_USED = [0] + list(range(T - 1, 0, -1))

    def strip_of(k, s):
        return s if k % 2 else (T - 1) - s

    def tri_index(k, s, u):
        return T * (T - 1) + (k - 2) * TRI + s * (s - 1) // 2 + u

    def stage_index(k, s):
        return T * s if k == 1 else T * T + (k - 2) * (TRI + T) + s * (s + 1) // 2

    def first_shared(k, s):
        return (T - 1) * s + T if k == 1 else stage_index(k, s) + 1

    def square_index(k, s):
        if k == 3:
            return s * (s - 1) // 2
        return TRI + (k - 4) * (TRI + T) + s * (s + 1) // 2

    def strips_before(k, s):
        return T * (k - 1) + s

    def over_strips(eng, k, strip):
        strip(k, 0)
        if k == 1 and T > 2:
            with eng.Fori(1, T - 1) as s:
                strip(k, s)
            strip(k, T - 1)
        else:
            with eng.Fori(1, T) as s:
                strip(k, s)

    def is_first(s):
        return isinstance(s, int) and s == 0

    def is_last(s):
        return isinstance(s, int) and s == T - 1

    with ExitStack() as ctx:
        def sb(name, shape, dt=F32):
            return ctx.enter_context(nc.sbuf_tensor(name, shape, dt))

        def ps(name, shape):
            return ctx.enter_context(nc.psum_tensor(name, shape, F32))

        def sem(name):
            return ctx.enter_context(nc.semaphore(name))

        diag = sb("diag", [P, NQ, 2, SW])
        tri = sb("tri", [P, NQ, 2, SW])
        sq = sb("sq", [P, NQ, 2, SW])
        row_sums = sq[:, 0]
        result = sq[:, :, :, :].rearrange("p q b i -> p (q b i)")[:, 0:T * NT * D].rearrange(
            "p (t d) -> p t d", d=D)
        vecs = sb("vecs", [P, NTILES, 2, D])
        resid = sb("resid", [P, NTILES, D])
        partial = sb("partial", [P, NTILES * P])
        stage = sb("stage", [P, 2, NT // 2, 2, D])
        alone_sb = sb("alone_sb", [P, SW])
        shared_sb = sb("shared_sb", [P, SW])
        new_x = sb("new_x", [P, NT, D])
        cen = sb("cen", [P, NT, D])
        cen2 = sb("cen2", [P, NT, D])
        small = sb("small", [P, 6, NT])
        degree = sb("degree", [P, NTILES])
        dinv = sb("dinv", [P, NTILES])
        dtmp = sb("dtmp", [P, 4, NTILES])
        w_top = sb("w_top", [P, SWEEPS, D])
        w_cat = sb("w_cat", [P, 2, D])
        bias_sb = sb("bias_sb", [P, 3, D])
        ident = sb("ident", [P, P])
        zeros = sb("zeros", [P, P], mybir.dt.bfloat16)
        ones = sb("ones", [P, 2])

        alone_ps = ps("alone_ps", [P, NI, BANK])
        shared_ps = ps("shared_ps", [P, NI, BANK])
        turn_ps = ps("turn_ps", [P, NI, BANK])
        post_ps = ps("post_ps", [P, BANK])
        deg_ps = ps("deg_ps", [P, BANK])

        x_loaded = [sem("x_loaded_first"), sem("x_loaded_rest")]
        w_loaded = sem("w_loaded")
        consts_set = sem("consts_set")
        diag_landed = [sem(f"diag_landed{q}") for q in range(NQ)]
        tri_landed = [sem(f"tri_landed{q}") for q in range(NQ)]
        diag_used = [sem(f"diag_used{q}") for q in range(NQ)]
        tri_used = [sem(f"tri_used{q}") for q in range(NQ)]
        sq_ready = [sem(f"sq_ready{q}") for q in range(NQ)]
        sq_free = [sem(f"sq_free{q}") for q in range(NQ)]
        stage_ready = [sem(f"stage_ready{j}") for j in range(2)]
        stage_free = [sem(f"stage_free{j}") for j in range(2)]
        vec_ready = sem("vec_ready")
        rows_added = sem("rows_added")
        deg_done = sem("deg_done")
        deg_copied = sem("deg_copied")
        alone_done = sem("alone_done")
        alone_copied = sem("alone_copied")
        shared_done = sem("shared_done")
        shared_copied = sem("shared_copied")
        partial_kept = sem("partial_kept")
        turned = sem("turned")
        turn_copied = sem("turn_copied")
        post_done = sem("post_done")
        tanh_ready = sem("tanh_ready")
        resid_kept = sem("resid_kept")
        STARTED = 1
        started = [deg_copied, resid_kept, *sq_free]
        step = sem("step")
        out_stored = sem("out_stored")

        turns_before = {1: 0, 2: T, 7: 2 * T}

        def computed(eng, *values):
            for v in values:
                if isinstance(v, bass.AP):
                    (eng.lower_ap_dma if v.tensor.name == adj.tensor.name else eng.lower_ap)(v)
                elif not isinstance(v, int):
                    eng.compute_val(v)

        def after(eng, sem, count):
            if not (isinstance(count, int) and count <= 0):
                eng.wait_ge(sem, count)

        def apart(eng):
            eng.wait_ge(consts_set, 1)

        block = ctx.enter_context(nc.Block())

        @block.sync
        def _(sp):
            for n, c in enumerate(FIRST_USED):
                sp.dma_start(resid[:, c * NT:(c + 1) * NT, :],
                             x[:, c * NT:(c + 1) * NT, :]).then_inc(x_loaded[min(n, 1)], 16)

            def load_d(k, s):
                i = strip_of(k, s)
                first = i * (T + 1) * NQ
                for q in range(NQ):
                    computed(sp, adj[first + q], strips_before(k, s),
                             NQ * T * (s - 1) + q + 1 if k == 1 else 0)
                    if not (k == 1 and is_first(s)):
                        sp.wait_ge(diag_used[q], strips_before(k, s))
                        if k == 1:
                            sp.wait_ge(rows_added, NQ * T * (s - 1) + q + 1)
                    sp.dma_start(diag[:, q].rearrange("p b i -> p (b i)"), adj[first + q]).then_inc(
                        diag_landed[q], 16)

            def load_t(k, i, j, n, added):
                first = (i * T + j) * NQ
                for q in range(NQ):
                    computed(sp, adj[first + q], n)
                    if added is not None:
                        sp.wait_ge(rows_added, added + q + 1)
                    after(sp, tri_used[q], n)
                    sp.dma_start(tri[:, q].rearrange("p b i -> p (b i)"), adj[first + q]).then_inc(
                        tri_landed[q], 16)

            def strip(k, s):
                i = strip_of(k, s)
                if k == 1 or not is_first(s):
                    load_d(k, s)
                if k == 1:
                    if not is_last(s):
                        if is_first(s):
                            load_t(k, i, T - 1, 0, None)
                        with sp.Fori(1 if is_first(s) else 0, T - 1 - s) as a:
                            load_t(k, i, (T - 1) - a, (T - 1) * s + a, NQ * (T * s + a))
                    if not is_first(s):
                        with sp.Fori(0, s) as j:
                            load_t(k, i, j, (T - 2) * s + (T - 1) + j,
                                   NQ * ((T - 1) * s + (T - 1) + j))
                elif not is_first(s):
                    with sp.Fori(0, s) as u:
                        load_t(k, i, strip_of(k, u), tri_index(k, s, u), None)

            for k in range(1, SWEEPS + 1):
                if k == 2:
                    sp.wait_ge(rows_added, NQ * T * T)
                over_strips(sp, k, strip)

        @block.gpsimd
        def _(pool):
            for c, count in enumerate(started):
                nc.gpsimd.memset(zeros[:, c * 16:(c + 1) * 16], 0.0).then_inc(count, STARTED)
            nc.gpsimd.memset(zeros[:, len(started) * 16:], 0.0)
            nc.gpsimd.memset(ones[:, :], 1.0).then_inc(consts_set, 1)
            pool.dma_start(ident[:, :], eye).then_inc(w_loaded, 16)
            for h in range(2):
                pool.dma_start(w_top[h * D:(h + 1) * D], wstack.rearrange("k a b -> a k b")).then_inc(
                    w_loaded, 16)
            pool.dma_start(w_cat[:, :, :], wcat.rearrange("k a b -> a k b")).then_inc(w_loaded, 16)
            pool.dma_start(bias_sb[:, :, :], bias).then_inc(w_loaded, 16)

            def put(j, n, half, strips=None):
                for h in range(2):
                    tiles = bass.ds(j * NT + h * (NT // 2), NT // 2)
                    computed(pool, n, *([] if strips is None else [strips]), vecs[:, tiles, 0 if half is None else half, :])
                    apart(pool)
                    after(pool, stage_free[h], n)
                    if strips is not None and h == 0:
                        pool.wait_ge(vec_ready, strips)
                    if half is None:
                        nc.gpsimd.tensor_copy(stage[:, h], vecs[:, tiles, :, :]).then_inc(
                            stage_ready[h], 1)
                    else:
                        nc.gpsimd.tensor_copy(stage[:, h, :, half, :],
                                              vecs[:, tiles, half, :]).then_inc(stage_ready[h], 1)

            def strip(k, s):
                f = (k - 1) % 2
                n = stage_index(k, s)
                if k == 1 and is_first(s):
                    pool.wait_ge(vec_ready, 1)
                elif is_first(s):
                    pool.wait_ge(vec_ready, T * k)
                put(strip_of(k, s), n, f)
                if k == 1 and not is_last(s):
                    with pool.Fori(0, T - 1 - s) as a:
                        put((T - 1) - a, n + 1 + a, f, strips=a + 2)
                if not is_first(s):
                    with pool.Fori(0, s) as u:
                        number = first_shared(k, s) + u
                        if k < SWEEPS:
                            put(strip_of(k, u), number, None, strips=T * k + u + 1)
                        else:
                            put(strip_of(k, u), number, f)

            for k in range(1, SWEEPS + 1):
                over_strips(pool, k, strip)

        @block.scalar
        def _(act):
            def square(q, src, landed, landings, m, squared):
                act.wait_ge(landed[q], landings)
                act.wait_ge(sq_free[q], STARTED + m)
                nc.scalar.activation(sq[:, q], src[:, q], ACT.Square).then_inc(squared[q], 1)

            def post(k, s):
                i = strip_of(k, s)
                act.wait_ge(post_done, strips_before(k, s) + 1)
                z = post_ps[:, :].rearrange("p (t d) -> p t d", d=D)
                if k == 1:
                    nc.scalar.activation(vecs[:, bass.ds(i * NT, NT), 1, :], z,
                                         ACT.Tanh).then_inc(vec_ready, 1)
                else:
                    act.wait_ge(resid_kept, STARTED + s)
                    nc.scalar.activation(new_x[:, :, :], z, ACT.Tanh).then_inc(tanh_ready, 1)

            def copy_turned(k, s):
                other = D * (k % 2)
                act.wait_ge(turned, turns_before[k] + s + 1)
                after(act, post_done, strips_before(k, s))
                nc.scalar.activation(shared_sb[other:other + D, :],
                                     turn_ps[other:other + D].rearrange("p b i -> p (b i)"),
                                     ACT.Copy).then_inc(turn_copied, 1)

            def strip(k, s):
                if k in TURNED:
                    if k < SWEEPS and not is_first(s):
                        post(k, s - 1)
                    copy_turned(k, s)
                if k in BY_SQUARE:
                    m = square_index(k, s)
                    for q in range(NQ):
                        square(q, diag, diag_landed, 16 * ((T - 1) * (k - 1) + s + 1), m, diag_used)
                if 3 <= k <= 6 and not is_first(s):
                    with act.Fori(0, s) as u:
                        m = square_index(k, s) + (0 if k == 3 else 1) + u
                        for q in range(NQ):
                            square(q, tri, tri_landed, 16 * (tri_index(k, s, u) + 1), m,
                                   tri_used if k in (4, 5) else sq_ready)
                if k == SWEEPS and not is_first(s):
                    store(s - 1)

            def store(s):
                act.wait_ge(vec_ready, strips_before(SWEEPS + 1, s) + 1)
                tiles = bass.ds(strip_of(SWEEPS, s) * NT, NT)
                act.dma_start(out[:, tiles, :], result[:, tiles, :]).then_inc(out_stored, 16)

            for k in range(1, SWEEPS + 1):
                if k == 3:
                    act.wait_ge(deg_done, T)
                over_strips(act, k, strip)
                if k < 3:
                    post(k, T - 1)
            store(T - 1)
            act.wait_ge(out_stored, 16 * T)

        @block.tensor
        def _(pe):
            def add_zero(bank, cols, **flags):
                return nc.tensor.matmul(bank[0:cols, 0:1], zeros[:, 0:cols], zeros[:, 0:1],
                                        skip_group_check=True, **flags)

            def alone(k, src, n, begins, ready, value, freed, turn):
                f = (k - 1) % 2
                other = D * (1 - f)
                for q in range(NQ):
                    h = q // 2
                    if q % 2 == 0:
                        pe.wait_ge(stage_ready[h], n + 1)
                    pe.wait_ge(ready[q], value)
                    for i in range(NI):
                        for b in range(2):
                            last = nc.tensor.matmul(
                                alone_ps[b * D:(b + 1) * D, i, :], stage[:, h, 2 * (q % 2) + b, f, :],
                                src[:, q, b, i * BANK:(i + 1) * BANK],
                                start=begins and q == 0, stop=False, skip_group_check=True)
                            if q == 2 and i == 0 and b == 0:
                                last.then_inc(stage_free[0], 1)
                    last.then_inc(freed[q], 1)
                    if q % 2 == 1 and turn:
                        for t in range(NT // 2):
                            last = nc.tensor.matmul(
                                turn_ps[other:other + D, h, t * P:(t + 1) * P],
                                stage[:, h, t, f, :], ident[:, :], start=True, stop=True)
                        if h == 1:
                            last.then_inc(turned, 1)
                add_zero(alone_ps[:, 0], D, start=False, stop=False).then_inc(stage_free[1], 1)

            def shared(k, n, n_tri, m):
                for q in range(NQ):
                    h = q // 2
                    if q % 2 == 0:
                        pe.wait_ge(stage_ready[h], n + 1)
                    if k in (1, 2, 3, 6):
                        pe.wait_ge(tri_landed[q], 16 * (n_tri + 1))
                    if k in (3, 6):
                        pe.wait_ge(sq_ready[q], m + 1)
                    if k in (4, 5):
                        pe.wait_ge(tri_used[q], n_tri + 1)
                    for b in range(2):
                        both = stage[:, h, 2 * (q % 2) + b].rearrange("p g d -> p (g d)")
                        for i in range(NI):
                            cols = slice(i * BANK, (i + 1) * BANK)
                            ends = b == 1 and i == NI - 1
                            if k in (3, 6):
                                of_a, of_w = [nc.tensor.matmul(
                                    shared_ps[g * D:(g + 1) * D, i, :], both[:, g * D:(g + 1) * D],
                                    src[:, q, b, cols], start=False, stop=False,
                                    skip_group_check=True) for g, src in enumerate((tri, sq))]
                                first = of_a
                                if ends:
                                    of_a.then_inc(tri_used[q], 1)
                                    of_w.then_inc(sq_free[q], 1)
                            else:
                                src, used = (tri, tri_used) if k < 3 else (sq, sq_free)
                                first = nc.tensor.matmul(shared_ps[:, i, :], both,
                                                         src[:, q, b, cols], start=False,
                                                         stop=False, skip_group_check=True)
                                if ends:
                                    first.then_inc(used[q], 1)
                            if q == 2 and b == 0 and i == 0:
                                first.then_inc(stage_free[0], 1)
                add_zero(shared_ps[:, 0], P, start=False, stop=False).then_inc(stage_free[1], 1)

            def bounds(bank, opens):
                for i in range(NI):
                    last = add_zero(bank[:, i], P, start=opens, stop=not opens)
                return last

            def post(k, s):
                f = (k - 1) % 2
                before = strips_before(k, s)
                pe.wait_ge(alone_copied, before + 1)
                pe.wait_ge(shared_copied, before + 1)
                if k in TURNED:
                    pe.wait_ge(turn_copied, turns_before[k] + s + 1)
                pe.wait_ge(vec_ready, T + before)
                rows = slice(0, P) if k in TURNED else slice(f * D, (f + 1) * D)
                w_shared = w_cat[:, k - 1, :] if k < 3 else w_top[rows, k - 1, :]
                for t in range(NT):
                    nc.tensor.matmul(post_ps[:, t * D:(t + 1) * D], alone_sb[:, t * P:(t + 1) * P],
                                     w_top[:, k - 1, :], start=True, stop=False)
                    last = nc.tensor.matmul(post_ps[:, t * D:(t + 1) * D],
                                            shared_sb[rows, t * P:(t + 1) * P], w_shared,
                                            start=False, stop=True)
                last.then_inc(post_done, 1)

            def sum_degrees(s):
                pe.wait_ge(rows_added, NQ * T * (s + 1))
                pe.wait_ge(deg_copied, STARTED + s)
                for t in range(NT):
                    for b in range(2):
                        last = nc.tensor.matmul(deg_ps[:, t:t + 1], row_sums[:, b, t * P:(t + 1) * P],
                                                ones[:, 0:1], start=b == 0, stop=b == 1)
                last.then_inc(deg_done, 1)

            def strip(k, s):
                n = stage_index(k, s)
                if k == 1 and not is_first(s):
                    sum_degrees(s - 1)
                after(pe, alone_copied, strips_before(k, s))
                if k in TURNED:
                    after(pe, turn_copied, turns_before[k] + s)
                if k in BY_SQUARE:
                    alone(k, sq, n, True, diag_used, strips_before(k, s) + 1, sq_free, False)
                else:
                    alone(k, diag, n, True, diag_landed, 16 * ((T - 1) * (k - 1) + s + 1), diag_used,
                          k in TURNED)
                if k == 2 and is_first(s):
                    sum_degrees(T - 1)
                if k == 1 and not is_last(s):
                    with pe.Fori(0, T - 1 - s) as a:
                        alone(k, tri, n + 1 + a, False, tri_landed, 16 * ((T - 1) * s + a + 1),
                              tri_used, False)
                if k < SWEEPS:
                    bounds(alone_ps, False).then_inc(alone_done, 1)
                if not is_first(s):
                    post(k, s - 1)
                    if k < SWEEPS:
                        pe.wait_ge(partial_kept, strips_before(k, s))
                        bounds(shared_ps, True)
                        with pe.Fori(0, s) as u:
                            if k == 1:
                                shared(k, first_shared(k, s) + u, (T - 2) * s + (T - 1) + u, None)
                            else:
                                m = (0 if k == 3 else TRI) + s * (s - 1) // 2 + u
                                shared(k, n + 1 + u, tri_index(k, s, u), m)
                        bounds(shared_ps, False).then_inc(shared_done, 1)
                    else:
                        with pe.Fori(0, s) as u:
                            alone(k, tri, n + 1 + u, False, tri_landed,
                                  16 * (tri_index(k, s, u) + 1), tri_used, False)
                if k == SWEEPS:
                    bounds(alone_ps, False).then_inc(alone_done, 1)

            pe.wait_ge(consts_set, 1)
            pe.wait_ge(w_loaded, 16 * 5)
            for k in range(1, SWEEPS + 1):
                over_strips(pe, k, strip)
                post(k, T - 1)

        @block.vector
        def _(dve):
            class Steps:
                def __init__(self, base):
                    self.base, self.n = base, 0

                def then(self, ins):
                    self.n += 1
                    ins.then_inc(step, 1)
                    dve.wait_ge(step, self.base + self.n)

            def spread(col, n=NT):
                return col.rearrange("p (t o) -> p t o", o=1).broadcast_to([P, n, D])

            def rsqrt(steps, y, v, t):
                steps.then(nc.vector.tensor_scalar(y.bitcast(I32), v.bitcast(I32), -0.5, RSQRT_GUESS,
                                                   ALU.mult, ALU.add))
                for _ in range(3):
                    steps.then(nc.vector.tensor_tensor(t, y, y, ALU.mult))
                    steps.then(nc.vector.scalar_tensor_tensor(out=t, in0=t, scalar=-0.5, in1=v,
                                                              op0=ALU.mult, op1=ALU.mult))
                    steps.then(nc.vector.scalar_tensor_tensor(out=y, in0=t, scalar=1.5, in1=y,
                                                              op0=ALU.add, op1=ALU.mult))

            def norm(steps, src, dst, scale=None):
                total, mean, var, t, y = (small[:, c, :] for c in range(5))
                steps.then(nc.vector.reduce_sum(total, src, AX))
                steps.then(nc.vector.tensor_scalar(mean, total, 1.0 / D, None, ALU.mult))
                steps.then(nc.vector.tensor_tensor(cen[:, :, :], src, spread(mean), ALU.subtract))
                steps.then(nc.vector.tensor_tensor(cen2[:, :, :], cen[:, :, :], cen[:, :, :],
                                                   ALU.mult))
                steps.then(nc.vector.reduce_sum(total, cen2[:, :, :], AX))
                steps.then(nc.vector.tensor_scalar(var, total, 1.0 / D, EPS, ALU.mult, ALU.add))
                rsqrt(steps, y, var, t)
                if scale is not None:
                    steps.then(nc.vector.tensor_tensor(y, y, scale, ALU.mult))
                nc.vector.scalar_tensor_tensor(out=dst, in0=cen[:, :, :], scalar=0.0, in1=spread(y),
                                               op0=ALU.max, op1=ALU.mult).then_inc(vec_ready, 1)

            def keep(x_i):
                nc.vector.tensor_copy(x_i, new_x[:, :, :]).then_inc(resid_kept, 1)

            KEPT_BEFORE = {2: 0, 3: T, 6: 2 * T, 7: 3 * T}
            POST_STEPS = {1: 0, 2: 17, 3: 21, 4: 0, 5: 0, 6: 19, 7: 1}
            steps_used = [0]

            def post(k, s):
                i = strip_of(k, s)
                tiles = bass.ds(i * NT, NT)
                z = post_ps[:, :].rearrange("p (t d) -> p t d", d=D)
                x_i = resid[:, tiles, :]
                v_next = vecs[:, tiles, k % 2, :]
                steps = Steps(steps_used[0] + POST_STEPS[k] * s)
                computed(dve, x_i, v_next, vecs[:, tiles, 0, :], dinv[:, tiles], result[:, tiles, :])
                if k == 2:
                    dve.wait_ge(tanh_ready, s + 1)
                else:
                    dve.wait_ge(post_done, strips_before(k, s) + 1)
                dve.wait_ge(vec_ready, strips_before(k + 1, s))
                if k in KEPT_BEFORE:
                    dve.wait_ge(resid_kept, STARTED + KEPT_BEFORE[k] + (s if k < SWEEPS else 0))
                if k == 2:
                    steps.then(nc.vector.tensor_tensor(new_x[:, :, :], new_x[:, :, :], x_i, ALU.add))
                    norm(steps, new_x[:, :, :], v_next)
                    keep(x_i)
                elif k == 3:
                    h = vecs[:, tiles, 0, :]
                    dot = small[:, 5, :]
                    mul = nc.vector.tensor_tensor(cen[:, :, :], z, h, ALU.mult)
                    steps.then(mul)
                    steps.then(nc.vector.reduce_sum(dot, cen[:, :, :], AX))
                    steps.then(nc.vector.tensor_scalar(dot, dot, -R_CONST, F_CONST, ALU.mult,
                                                       ALU.add))
                    steps.then(nc.vector.scalar_tensor_tensor(out=cen2[:, :, :], in0=h,
                                                              scalar=-B_CONST, in1=spread(dot),
                                                              op0=ALU.mult, op1=ALU.add))
                    steps.then(nc.vector.tensor_tensor(new_x[:, :, :], x_i, cen2[:, :, :], ALU.add))
                    norm(steps, new_x[:, :, :], v_next)
                    keep(x_i)
                elif k in (4, 5):
                    b = bias_sb[:, k - 4:k - 3, :].broadcast_to([P, NT, D])
                    add = nc.vector.tensor_tensor(v_next, z, b, ALU.add)
                    add.then_inc(vec_ready, 1)
                elif k == 6:
                    b = bias_sb[:, 2:3, :].broadcast_to([P, NT, D])
                    add = nc.vector.tensor_tensor(cen[:, :, :], z, b, ALU.add)
                    steps.then(add)
                    steps.then(nc.vector.tensor_tensor(new_x[:, :, :], x_i, cen[:, :, :], ALU.add))
                    norm(steps, new_x[:, :, :], v_next, scale=dinv[:, tiles])
                    keep(x_i)
                elif k == 7:
                    mul = nc.vector.tensor_tensor(cen[:, :, :], z, spread(dinv[:, tiles]), ALU.mult)
                    steps.then(mul)
                    nc.vector.tensor_tensor(result[:, tiles, :], x_i, cen[:, :, :],
                                            ALU.add).then_inc(vec_ready, 1)
                assert k == 1 or steps.n == POST_STEPS[k], (k, steps.n)

            def copy_alone(k, s):
                dve.wait_ge(alone_done, strips_before(k, s) + 1)
                after(dve, post_done, strips_before(k, s))
                nc.vector.tensor_copy(alone_sb[:, :], alone_ps[:, :, :].rearrange(
                    "p b i -> p (b i)")).then_inc(alone_copied, 1)

            def copy_shared(k, s):
                i = strip_of(k, s)
                fin = slice(D * ((k - 1) % 2), D * ((k - 1) % 2) + D)
                beg = slice(D * (k % 2), D * (k % 2) + D)
                cols = bass.ds(i * SW, SW)
                banks = shared_ps[:, :, :].rearrange("p b i -> p (b i)")
                computed(dve, partial[fin, cols], partial[beg, cols])
                if is_first(s) or k == SWEEPS:
                    if k > 1:
                        apart(dve)
                    after(dve, post_done, strips_before(k, s))
                    if k == 1:
                        nc.vector.memset(shared_sb[fin, :], 0.0).then_inc(shared_copied, 1)
                    else:
                        nc.vector.tensor_copy(shared_sb[fin, :], partial[fin, cols]).then_inc(
                            shared_copied, 1)
                    if k < SWEEPS:
                        nc.vector.memset(partial[beg, cols], 0.0).then_inc(partial_kept, 1)
                    return
                dve.wait_ge(shared_done, (T - 1) * (k - 1) + s)
                if k == 1:
                    nc.vector.tensor_copy(shared_sb[fin, :], banks[fin]).then_inc(shared_copied, 1)
                else:
                    nc.vector.tensor_tensor(shared_sb[fin, :], banks[fin], partial[fin, cols],
                                            ALU.add).then_inc(shared_copied, 1)
                nc.vector.tensor_copy(partial[beg, cols], banks[beg]).then_inc(partial_kept, 1)

            def add_rows(src, landed, landings, n, begins=False):
                for q in range(NQ):
                    dve.wait_ge(landed[q], landings)
                    if begins and q == 0:
                        nc.vector.tensor_copy(row_sums, src[:, q]).then_inc(rows_added, 1)
                        continue
                    dve.wait_ge(rows_added, NQ * n + q)
                    nc.vector.tensor_tensor(row_sums, row_sums, src[:, q], ALU.add).then_inc(
                        rows_added, 1)

            def copy_degrees(s):
                dve.wait_ge(deg_done, s + 1)
                nc.vector.tensor_copy(degree[:, bass.ds(s * NT, NT)], deg_ps[:, 0:NT]).then_inc(
                    deg_copied, 1)

            def inverse_roots():
                steps = Steps(steps_used[0])
                deg, floor, y, t = (dtmp[:, c, :] for c in range(4))
                dve.wait_ge(deg_copied, STARTED + T)
                steps.then(nc.vector.tensor_scalar(deg, degree[:, :], 1.0, None, ALU.add))
                steps.then(nc.vector.tensor_scalar(floor, deg, TINY, None, ALU.max))
                rsqrt(steps, y, floor, t)
                steps.then(nc.vector.scalar_tensor_tensor(out=dinv[:, :], in0=deg, scalar=0.0, in1=y,
                                                          op0=ALU.is_gt, op1=ALU.mult))
                steps_used[0] += steps.n

            def strip(k, s):
                if k == 1:
                    if not is_first(s):
                        copy_degrees(s - 1)
                    add_rows(diag, diag_landed, 16 * (s + 1), T * s, begins=True)
                    if not is_last(s):
                        with dve.Fori(0, T - 1 - s) as a:
                            add_rows(tri, tri_landed, 16 * ((T - 1) * s + a + 1), T * s + 1 + a)
                    if is_first(s):
                        copy_shared(k, s)
                    copy_alone(k, s)
                    if not is_first(s):
                        with dve.Fori(0, s) as j:
                            add_rows(tri, tri_landed, 16 * ((T - 2) * s + T + j),
                                     (T - 1) * s + T + j)
                        copy_shared(k, s)
                    return
                if not is_first(s):
                    post(k, s - 1)
                if is_first(s) or k == SWEEPS:
                    copy_shared(k, s)
                    copy_alone(k, s)
                else:
                    copy_alone(k, s)
                    copy_shared(k, s)
                if k == 2 and is_first(s):
                    copy_degrees(T - 1)
                    inverse_roots()

            for n, c in enumerate(FIRST_USED):
                tiles = slice(c * NT, (c + 1) * NT)
                if n < 2:
                    dve.wait_ge(x_loaded[n], 16 if n == 0 else 16 * (T - 1))
                if n:
                    dve.wait_ge(vec_ready, n)
                steps = Steps(steps_used[0])
                norm(steps, resid[:, tiles, :], vecs[:, tiles, 0, :])
                steps_used[0] += steps.n
            dve.wait_ge(w_loaded, 16 * 5)
            for k in range(1, SWEEPS + 1):
                if k > 1:
                    dve.wait_ge(partial_kept, T * (k - 1))
                over_strips(dve, k, strip)
                if k > 1:
                    post(k, T - 1)
                    steps_used[0] += POST_STEPS[k] * T


def kernel(x, adj, L0_gnn_W, L1_gnn_t, L2_gnn_W0, L2_gnn_b0, L2_gnn_W1, L2_gnn_b1, L2_gnn_W2,
           L2_gnn_b2, L3_gnn_W):
    import numpy as np
    import concourse.bacc as bacc
    from concourse import mybir as mb
    from concourse.bass_utils import run_bass_kernel_spmd

    n = x.shape[0]
    t = n // SW
    a = {}
    a["x_rows"] = np.ascontiguousarray(np.asarray(x).reshape(n // P, P, D).transpose(1, 0, 2))
    a["adj_units"] = np.ascontiguousarray(
        np.asarray(adj).reshape(t, SW, t, NQ, 2, P).transpose(0, 2, 3, 5, 4, 1)).reshape(
            t * t * NQ, P, 2 * SW)
    w0 = np.asarray(L0_gnn_W)
    eye = np.eye(P, dtype=np.float32)
    a["w_right"] = np.stack([w0[0, :D], w0[1, :D], eye[:D, :D], np.asarray(L2_gnn_W0).T,
                             np.asarray(L2_gnn_W1).T, np.asarray(L2_gnn_W2).T, np.asarray(L3_gnn_W)])
    a["w_concat"] = np.stack([w0[0], np.concatenate([w0[1, D:], w0[1, :D]])])
    a["bias_rows"] = np.ascontiguousarray(np.broadcast_to(
        np.stack([np.asarray(b) for b in (L2_gnn_b0, L2_gnn_b1, L2_gnn_b2)]), (P, 3, D)))
    a["eye"] = eye
    nc = bacc.Bacc("TRN2", target_bir_lowering=False, num_devices=1)
    aps = [nc.dram_tensor(name, v.shape, mb.dt.float32, kind="ExternalInput").ap()
           for name, v in a.items()]
    out = nc.dram_tensor("out_rows", a["x_rows"].shape, mb.dt.float32, kind="ExternalOutput").ap()
    graph_layers(nc, *aps, out)
    r = run_bass_kernel_spmd(nc, [a], core_ids=[0])
    rows = r.results[0]["out_rows"]
    return np.ascontiguousarray(rows.transpose(1, 0, 2)).reshape(n, D)
```

```python
from contextlib import ExitStack

import concourse.bass as bass
from concourse import mybir

F32 = mybir.dt.float32
I32 = mybir.dt.int32
ALU = mybir.AluOpType
ACT = mybir.ActivationFunctionType
AX = mybir.AxisListType.X

P = 128
D = 64
SW = 1024
NT = SW // P
NQ = 4
BANK = 512
NI = SW // BANK
SWEEPS = 7
EPS = 1e-5
F_CONST, B_CONST, R_CONST = 1.0, 0.1, 0.01
TINY = 1.1754944e-38
RSQRT_GUESS = float(0x5F3759DF)
TURNED = (1, 2, 7)
BY_SQUARE = (4, 5, 6)


def graph_layers(nc, x, adj, wstack, wcat, bias, eye, out):
    NTILES = x.shape[1]
    T = NTILES // NT
    assert adj.shape[0] == T * T * NQ and T >= 4 and T % 2 == 0
    TRI = T * (T - 1) // 2
    FIRST_USED = [0] + list(range(T - 1, 0, -1))

    def strip_of(k, s):
        return s if k % 2 else (T - 1) - s

    def tri_index(k, s, u):
        return T * (T - 1) + (k - 2) * TRI + s * (s - 1) // 2 + u

    def stage_index(k, s):
        return T * s if k == 1 else T * T + (k - 2) * (TRI + T) + s * (s + 1) // 2

    def square_index(k, s):
        if k == 3:
            return s * (s - 1) // 2
        return TRI + (k - 4) * (TRI + T) + s * (s + 1) // 2

    def strips_before(k, s):
        return T * (k - 1) + s

    def over_strips(eng, k, strip):
        strip(k, 0)
        if k > 1:
            with eng.Fori(1, T) as s:
                strip(k, s)
            return
        with eng.Fori(1, T // 2) as s:
            strip(k, s, early=True)
        with eng.Fori(T // 2, T - 1) as s:
            strip(k, s)
        strip(k, T - 1)

    def sweep_one(eng, s, early, alone, shared, lower_opens, upper_ends):
        if is_first(s):
            with eng.Fori(0, T - 1) as a:
                alone(T * s + 1 + a, (T - 1) * s + a, (T - 1) - a)
            upper_ends()
        elif early:
            with eng.Fori(0, T - 1 - 2 * s) as a:
                alone(T * s + 1 + a, (T - 1) * s + a, (T - 1) - a)
            lower_opens()
            with eng.Fori(0, s) as b:
                alone((T - 2) * s + T + 2 * b, (T - 3) * s + (T - 1) + 2 * b, 2 * s - b)
                shared((T - 2) * s + T + 1 + 2 * b, (T - 3) * s + T + 2 * b, b)
            upper_ends()
        elif is_last(s):
            upper_ends()
            lower_opens()
            with eng.Fori(0, s) as b:
                shared(T * s + 1 + b, (T - 1) * s + b, b)
        else:
            lower_opens()
            with eng.Fori(0, T - 1 - s) as b:
                alone(T * s + 1 + 2 * b, (T - 1) * s + 2 * b, (T - 1) - b)
                shared(T * s + 2 + 2 * b, (T - 1) * s + 1 + 2 * b, b)
            upper_ends()
            with eng.Fori(0, 2 * s - (T - 1)) as c:
                shared((T - 2) * s + (2 * T - 1) + c, (T - 3) * s + (2 * T - 2) + c, (T - 1) - s + c)

    def is_first(s):
        return isinstance(s, int) and s == 0

    def is_last(s):
        return isinstance(s, int) and s == T - 1

    with ExitStack() as ctx:
        def sb(name, shape, dt=F32):
            return ctx.enter_context(nc.sbuf_tensor(name, shape, dt))

        def ps(name, shape):
            return ctx.enter_context(nc.psum_tensor(name, shape, F32))

        def sem(name):
            return ctx.enter_context(nc.semaphore(name))

        diag = sb("diag", [P, NQ, 2, SW])
        tri = sb("tri", [P, NQ, 2, SW])
        sq = sb("sq", [P, NQ, 2, SW])
        row_sums = sq[:, 0]
        result = sq[:, :, :, :].rearrange("p q b i -> p (q b i)")[:, 0:T * NT * D].rearrange(
            "p (t d) -> p t d", d=D)
        vecs = sb("vecs", [P, NTILES, 2, D])
        resid = sb("resid", [P, NTILES, D])
        partial = sb("partial", [P, NTILES * P])
        stage = sb("stage", [P, 2, NT // 2, 2, D])
        alone_sb = sb("alone_sb", [P, SW])
        shared_sb = sb("shared_sb", [P, SW])
        new_x = sb("new_x", [P, NT, D])
        cen = sb("cen", [P, NT, D])
        cen2 = sb("cen2", [P, NT, D])
        small = sb("small", [P, 6, NT])
        degree = sb("degree", [P, NTILES])
        dinv = sb("dinv", [P, NTILES])
        dtmp = sb("dtmp", [P, 4, NTILES])
        w_top = sb("w_top", [P, SWEEPS, D])
        w_cat = sb("w_cat", [P, 2, D])
        bias_sb = sb("bias_sb", [P, 3, D])
        ident = sb("ident", [P, P])
        zeros = sb("zeros", [P, P], mybir.dt.bfloat16)
        ones = sb("ones", [P, 2])

        alone_ps = ps("alone_ps", [P, NI, BANK])
        shared_ps = ps("shared_ps", [P, NI, BANK])
        turn_ps = ps("turn_ps", [P, NI, BANK])
        post_ps = ps("post_ps", [P, BANK])
        deg_ps = ps("deg_ps", [P, BANK])

        x_loaded = [sem("x_loaded_first"), sem("x_loaded_rest")]
        w_loaded = sem("w_loaded")
        consts_set = sem("consts_set")
        diag_landed = [sem(f"diag_landed{q}") for q in range(NQ)]
        tri_landed = [sem(f"tri_landed{q}") for q in range(NQ)]
        diag_used = [sem(f"diag_used{q}") for q in range(NQ)]
        tri_used = [sem(f"tri_used{q}") for q in range(NQ)]
        sq_ready = [sem(f"sq_ready{q}") for q in range(NQ)]
        sq_free = [sem(f"sq_free{q}") for q in range(NQ)]
        stage_ready = [sem(f"stage_ready{j}") for j in range(2)]
        stage_free = [sem(f"stage_free{j}") for j in range(2)]
        vec_ready = sem("vec_ready")
        rows_added = sem("rows_added")
        deg_done = sem("deg_done")
        deg_copied = sem("deg_copied")
        alone_done = sem("alone_done")
        alone_copied = sem("alone_copied")
        shared_done = sem("shared_done")
        shared_copied = sem("shared_copied")
        partial_kept = sem("partial_kept")
        turned = sem("turned")
        turn_copied = sem("turn_copied")
        post_done = sem("post_done")
        tanh_ready = sem("tanh_ready")
        resid_kept = sem("resid_kept")
        STARTED = 1
        started = [deg_copied, resid_kept, *sq_free]
        step = sem("step")
        out_stored = sem("out_stored")

        turns_before = {1: 0, 2: T, 7: 2 * T}

        def computed(eng, *values):
            for v in values:
                if isinstance(v, bass.AP):
                    (eng.lower_ap_dma if v.tensor.name == adj.tensor.name else eng.lower_ap)(v)
                elif not isinstance(v, int):
                    eng.compute_val(v)

        def after(eng, sem, count):
            if not (isinstance(count, int) and count <= 0):
                eng.wait_ge(sem, count)

        def apart(eng):
            eng.wait_ge(consts_set, 1)

        block = ctx.enter_context(nc.Block())

        @block.sync
        def _(sp):
            for n, c in enumerate(FIRST_USED):
                sp.dma_start(resid[:, c * NT:(c + 1) * NT, :],
                             x[:, c * NT:(c + 1) * NT, :]).then_inc(x_loaded[min(n, 1)], 16)

            def load_d(k, s):
                i = strip_of(k, s)
                first = i * (T + 1) * NQ
                for q in range(NQ):
                    computed(sp, adj[first + q], strips_before(k, s),
                             NQ * T * (s - 1) + q + 1 if k == 1 else 0)
                    if not (k == 1 and is_first(s)):
                        sp.wait_ge(diag_used[q], strips_before(k, s))
                        if k == 1:
                            sp.wait_ge(rows_added, NQ * T * (s - 1) + q + 1)
                    sp.dma_start(diag[:, q].rearrange("p b i -> p (b i)"), adj[first + q]).then_inc(
                        diag_landed[q], 16)

            def load_t(k, i, j, n, added):
                first = (i * T + j) * NQ
                for q in range(NQ):
                    computed(sp, adj[first + q], n)
                    if added is not None:
                        sp.wait_ge(rows_added, added + q + 1)
                    after(sp, tri_used[q], n)
                    sp.dma_start(tri[:, q].rearrange("p b i -> p (b i)"), adj[first + q]).then_inc(
                        tri_landed[q], 16)

            def strip(k, s, early=False):
                i = strip_of(k, s)
                if k == 1 or not is_first(s):
                    load_d(k, s)
                if k == 1:
                    def load(place, n, j):
                        load_t(k, i, j, n, NQ * (place - 1))
                    sweep_one(sp, s, early, load, load, lambda: None, lambda: None)
                elif not is_first(s):
                    with sp.Fori(0, s) as u:
                        load_t(k, i, strip_of(k, u), tri_index(k, s, u), None)

            for k in range(1, SWEEPS + 1):
                if k == 2:
                    sp.wait_ge(rows_added, NQ * T * T)
                over_strips(sp, k, strip)

        @block.gpsimd
        def _(pool):
            for c, count in enumerate(started):
                nc.gpsimd.memset(zeros[:, c * 16:(c + 1) * 16], 0.0).then_inc(count, STARTED)
            nc.gpsimd.memset(zeros[:, len(started) * 16:], 0.0)
            nc.gpsimd.memset(ones[:, :], 1.0).then_inc(consts_set, 1)
            pool.dma_start(ident[:, :], eye).then_inc(w_loaded, 16)
            for h in range(2):
                pool.dma_start(w_top[h * D:(h + 1) * D], wstack.rearrange("k a b -> a k b")).then_inc(
                    w_loaded, 16)
            pool.dma_start(w_cat[:, :, :], wcat.rearrange("k a b -> a k b")).then_inc(w_loaded, 16)
            pool.dma_start(bias_sb[:, :, :], bias).then_inc(w_loaded, 16)

            def put(j, n, half, strips=None):
                for h in range(2):
                    tiles = bass.ds(j * NT + h * (NT // 2), NT // 2)
                    computed(pool, n, *([] if strips is None else [strips]), vecs[:, tiles, 0 if half is None else half, :])
                    apart(pool)
                    after(pool, stage_free[h], n)
                    if strips is not None and h == 0:
                        pool.wait_ge(vec_ready, strips)
                    if half is None:
                        nc.gpsimd.tensor_copy(stage[:, h], vecs[:, tiles, :, :]).then_inc(
                            stage_ready[h], 1)
                    else:
                        nc.gpsimd.tensor_copy(stage[:, h, :, half, :],
                                              vecs[:, tiles, half, :]).then_inc(stage_ready[h], 1)

            def strip(k, s, early=False):
                f = (k - 1) % 2
                n = stage_index(k, s)
                if k == 1 and is_first(s):
                    pool.wait_ge(vec_ready, 1)
                elif is_first(s):
                    pool.wait_ge(vec_ready, T * k)
                put(strip_of(k, s), n, f)
                if k == 1:
                    sweep_one(pool, s, early,
                              lambda place, _, j: put(j, place, f,
                                                      strips=place + 1 if is_first(s) else None),
                              lambda place, _, j: put(
                                  j, place, None, strips=T + (j + 1 if is_last(s) else s)),
                              lambda: None, lambda: None)
                elif not is_first(s):
                    with pool.Fori(0, s) as u:
                        if k < SWEEPS:
                            put(strip_of(k, u), n + 1 + u, None, strips=T * k + u + 1)
                        else:
                            put(strip_of(k, u), n + 1 + u, f)

            for k in range(1, SWEEPS + 1):
                over_strips(pool, k, strip)

        @block.scalar
        def _(act):
            def square(q, src, landed, landings, m, squared):
                act.wait_ge(landed[q], landings)
                act.wait_ge(sq_free[q], STARTED + m)
                nc.scalar.activation(sq[:, q], src[:, q], ACT.Square).then_inc(squared[q], 1)

            def post(k, s):
                i = strip_of(k, s)
                act.wait_ge(post_done, strips_before(k, s) + 1)
                z = post_ps[:, :].rearrange("p (t d) -> p t d", d=D)
                if k == 1:
                    nc.scalar.activation(vecs[:, bass.ds(i * NT, NT), 1, :], z,
                                         ACT.Tanh).then_inc(vec_ready, 1)
                else:
                    act.wait_ge(resid_kept, STARTED + s)
                    nc.scalar.activation(new_x[:, :, :], z, ACT.Tanh).then_inc(tanh_ready, 1)

            def copy_turned(k, s):
                other = D * (k % 2)
                act.wait_ge(turned, turns_before[k] + s + 1)
                after(act, post_done, strips_before(k, s))
                nc.scalar.activation(shared_sb[other:other + D, :],
                                     turn_ps[other:other + D].rearrange("p b i -> p (b i)"),
                                     ACT.Copy).then_inc(turn_copied, 1)

            def strip(k, s, early=False):
                if k in TURNED:
                    if k < SWEEPS and not is_first(s):
                        post(k, s - 1)
                    copy_turned(k, s)
                if k in BY_SQUARE:
                    m = square_index(k, s)
                    for q in range(NQ):
                        square(q, diag, diag_landed, 16 * ((T - 1) * (k - 1) + s + 1), m, diag_used)
                if 3 <= k <= 6 and not is_first(s):
                    with act.Fori(0, s) as u:
                        m = square_index(k, s) + (0 if k == 3 else 1) + u
                        for q in range(NQ):
                            square(q, tri, tri_landed, 16 * (tri_index(k, s, u) + 1), m,
                                   tri_used if k in (4, 5) else sq_ready)
                if k == SWEEPS and not is_first(s):
                    store(s - 1)

            def store(s):
                act.wait_ge(vec_ready, strips_before(SWEEPS + 1, s) + 1)
                tiles = bass.ds(strip_of(SWEEPS, s) * NT, NT)
                act.dma_start(out[:, tiles, :], result[:, tiles, :]).then_inc(out_stored, 16)

            for k in range(1, SWEEPS + 1):
                if k == 3:
                    act.wait_ge(deg_done, T)
                over_strips(act, k, strip)
                if k < 3:
                    post(k, T - 1)
            store(T - 1)
            act.wait_ge(out_stored, 16 * T)

        @block.tensor
        def _(pe):
            def add_zero(bank, cols, **flags):
                return nc.tensor.matmul(bank[0:cols, 0:1], zeros[:, 0:cols], zeros[:, 0:1],
                                        skip_group_check=True, **flags)

            def alone(k, src, n, begins, ready, value, freed, turn):
                f = (k - 1) % 2
                other = D * (1 - f)
                for q in range(NQ):
                    h = q // 2
                    if q % 2 == 0:
                        pe.wait_ge(stage_ready[h], n + 1)
                    pe.wait_ge(ready[q], value)
                    for i in range(NI):
                        for b in range(2):
                            last = nc.tensor.matmul(
                                alone_ps[b * D:(b + 1) * D, i, :], stage[:, h, 2 * (q % 2) + b, f, :],
                                src[:, q, b, i * BANK:(i + 1) * BANK],
                                start=begins and q == 0, stop=False, skip_group_check=True)
                            if q == 2 and i == 0 and b == 0:
                                last.then_inc(stage_free[0], 1)
                    last.then_inc(freed[q], 1)
                    if q % 2 == 1 and turn:
                        for t in range(NT // 2):
                            last = nc.tensor.matmul(
                                turn_ps[other:other + D, h, t * P:(t + 1) * P],
                                stage[:, h, t, f, :], ident[:, :], start=True, stop=True)
                        if h == 1:
                            last.then_inc(turned, 1)
                add_zero(alone_ps[:, 0], D, start=False, stop=False).then_inc(stage_free[1], 1)

            def shared(k, n, n_tri, m):
                for q in range(NQ):
                    h = q // 2
                    if q % 2 == 0:
                        pe.wait_ge(stage_ready[h], n + 1)
                    if k in (1, 2, 3, 6):
                        pe.wait_ge(tri_landed[q], 16 * (n_tri + 1))
                    if k in (3, 6):
                        pe.wait_ge(sq_ready[q], m + 1)
                    if k in (4, 5):
                        pe.wait_ge(tri_used[q], n_tri + 1)
                    for b in range(2):
                        both = stage[:, h, 2 * (q % 2) + b].rearrange("p g d -> p (g d)")
                        for i in range(NI):
                            cols = slice(i * BANK, (i + 1) * BANK)
                            ends = b == 1 and i == NI - 1
                            if k in (3, 6):
                                of_a, of_w = [nc.tensor.matmul(
                                    shared_ps[g * D:(g + 1) * D, i, :], both[:, g * D:(g + 1) * D],
                                    src[:, q, b, cols], start=False, stop=False,
                                    skip_group_check=True) for g, src in enumerate((tri, sq))]
                                first = of_a
                                if ends:
                                    of_a.then_inc(tri_used[q], 1)
                                    of_w.then_inc(sq_free[q], 1)
                            else:
                                src, used = (tri, tri_used) if k < 3 else (sq, sq_free)
                                first = nc.tensor.matmul(shared_ps[:, i, :], both,
                                                         src[:, q, b, cols], start=False,
                                                         stop=False, skip_group_check=True)
                                if ends:
                                    first.then_inc(used[q], 1)
                            if q == 2 and b == 0 and i == 0:
                                first.then_inc(stage_free[0], 1)
                add_zero(shared_ps[:, 0], P, start=False, stop=False).then_inc(stage_free[1], 1)

            def bounds(bank, opens):
                for i in range(NI):
                    last = add_zero(bank[:, i], P, start=opens, stop=not opens)
                return last

            def post(k, s):
                before = strips_before(k, s)
                pe.wait_ge(alone_copied, before + 1)
                pe.wait_ge(shared_copied, before + 1)
                if k in TURNED:
                    pe.wait_ge(turn_copied, turns_before[k] + s + 1)
                pe.wait_ge(vec_ready, T + before)
                for t in range(NT):
                    last = nc.tensor.matmul(post_ps[:, t * D:(t + 1) * D],
                                            alone_sb[:, t * P:(t + 1) * P], w_top[:, k - 1, :],
                                            start=True, stop=k not in TURNED)
                    if k in TURNED:
                        last = nc.tensor.matmul(post_ps[:, t * D:(t + 1) * D],
                                                shared_sb[:, t * P:(t + 1) * P],
                                                w_cat[:, k - 1, :] if k < 3 else w_top[:, k - 1, :],
                                                start=False, stop=True)
                last.then_inc(post_done, 1)

            def sum_degrees(s):
                pe.wait_ge(rows_added, NQ * T * (s + 1))
                pe.wait_ge(deg_copied, STARTED + s)
                for t in range(NT):
                    for b in range(2):
                        last = nc.tensor.matmul(deg_ps[:, t:t + 1], row_sums[:, b, t * P:(t + 1) * P],
                                                ones[:, 0:1], start=b == 0, stop=b == 1)
                last.then_inc(deg_done, 1)

            def strip(k, s, early=False):
                n = stage_index(k, s)
                if k == 1 and not is_first(s):
                    sum_degrees(s - 1)
                after(pe, alone_copied, strips_before(k, s))
                if k in TURNED:
                    after(pe, turn_copied, turns_before[k] + s)
                if k in BY_SQUARE:
                    alone(k, sq, n, True, diag_used, strips_before(k, s) + 1, sq_free, False)
                else:
                    alone(k, diag, n, True, diag_landed, 16 * ((T - 1) * (k - 1) + s + 1), diag_used,
                          k in TURNED)
                if k == 2 and is_first(s):
                    sum_degrees(T - 1)
                def open_shared():
                    after(pe, partial_kept, strips_before(k, s))
                    bounds(shared_ps, True)

                def end_alone():
                    bounds(alone_ps, False).then_inc(alone_done, 1)

                if k == 1:
                    def begin_lower():
                        post(k, s - 1)
                        open_shared()

                    sweep_one(pe, s, early,
                              lambda place, n_tri, _: alone(k, tri, place, False, tri_landed,
                                                            16 * (n_tri + 1), tri_used, False),
                              lambda place, n_tri, _: shared(k, place, n_tri, None),
                              begin_lower, end_alone)
                elif k < SWEEPS:
                    end_alone()
                    if not is_first(s):
                        post(k, s - 1)
                        open_shared()
                        with pe.Fori(0, s) as u:
                            m = (0 if k == 3 else TRI) + s * (s - 1) // 2 + u
                            shared(k, n + 1 + u, tri_index(k, s, u), m)
                else:
                    if not is_first(s):
                        post(k, s - 1)
                        with pe.Fori(0, s) as u:
                            alone(k, tri, n + 1 + u, False, tri_landed,
                                  16 * (tri_index(k, s, u) + 1), tri_used, False)
                    end_alone()
                if k < SWEEPS and not is_first(s):
                    bounds(shared_ps, False).then_inc(shared_done, 1)

            pe.wait_ge(consts_set, 1)
            pe.wait_ge(w_loaded, 16 * 5)
            for k in range(1, SWEEPS + 1):
                over_strips(pe, k, strip)
                post(k, T - 1)

        @block.vector
        def _(dve):
            class Steps:
                def __init__(self, base):
                    self.base, self.n = base, 0

                def then(self, ins):
                    self.n += 1
                    ins.then_inc(step, 1)
                    dve.wait_ge(step, self.base + self.n)

            def spread(col, n=NT):
                return col.rearrange("p (t o) -> p t o", o=1).broadcast_to([P, n, D])

            def rsqrt(steps, y, v, t):
                steps.then(nc.vector.tensor_scalar(y.bitcast(I32), v.bitcast(I32), -0.5, RSQRT_GUESS,
                                                   ALU.mult, ALU.add))
                for _ in range(3):
                    steps.then(nc.vector.tensor_tensor(t, y, y, ALU.mult))
                    steps.then(nc.vector.scalar_tensor_tensor(out=t, in0=t, scalar=-0.5, in1=v,
                                                              op0=ALU.mult, op1=ALU.mult))
                    steps.then(nc.vector.scalar_tensor_tensor(out=y, in0=t, scalar=1.5, in1=y,
                                                              op0=ALU.add, op1=ALU.mult))

            def norm(steps, src, dst, scale=None):
                total, mean, var, t, y = (small[:, c, :] for c in range(5))
                steps.then(nc.vector.reduce_sum(total, src, AX))
                steps.then(nc.vector.tensor_scalar(mean, total, 1.0 / D, None, ALU.mult))
                steps.then(nc.vector.tensor_tensor(cen[:, :, :], src, spread(mean), ALU.subtract))
                steps.then(nc.vector.tensor_tensor(cen2[:, :, :], cen[:, :, :], cen[:, :, :],
                                                   ALU.mult))
                steps.then(nc.vector.reduce_sum(total, cen2[:, :, :], AX))
                steps.then(nc.vector.tensor_scalar(var, total, 1.0 / D, EPS, ALU.mult, ALU.add))
                rsqrt(steps, y, var, t)
                if scale is not None:
                    steps.then(nc.vector.tensor_tensor(y, y, scale, ALU.mult))
                nc.vector.scalar_tensor_tensor(out=dst, in0=cen[:, :, :], scalar=0.0, in1=spread(y),
                                               op0=ALU.max, op1=ALU.mult).then_inc(vec_ready, 1)

            def keep(x_i):
                nc.vector.tensor_copy(x_i, new_x[:, :, :]).then_inc(resid_kept, 1)

            KEPT_BEFORE = {2: 0, 3: T, 6: 2 * T, 7: 3 * T}
            POST_STEPS = {1: 0, 2: 17, 3: 21, 4: 0, 5: 0, 6: 19, 7: 1}
            steps_used = [0]

            def post(k, s):
                i = strip_of(k, s)
                tiles = bass.ds(i * NT, NT)
                z = post_ps[:, :].rearrange("p (t d) -> p t d", d=D)
                x_i = resid[:, tiles, :]
                v_next = vecs[:, tiles, k % 2, :]
                steps = Steps(steps_used[0] + POST_STEPS[k] * s)
                computed(dve, x_i, v_next, vecs[:, tiles, 0, :], dinv[:, tiles], result[:, tiles, :])
                if k == 2:
                    dve.wait_ge(tanh_ready, s + 1)
                else:
                    dve.wait_ge(post_done, strips_before(k, s) + 1)
                dve.wait_ge(vec_ready, strips_before(k + 1, s))
                if k in KEPT_BEFORE:
                    dve.wait_ge(resid_kept, STARTED + KEPT_BEFORE[k] + (s if k < SWEEPS else 0))
                if k == 2:
                    steps.then(nc.vector.tensor_tensor(new_x[:, :, :], new_x[:, :, :], x_i, ALU.add))
                    norm(steps, new_x[:, :, :], v_next)
                    keep(x_i)
                elif k == 3:
                    h = vecs[:, tiles, 0, :]
                    dot = small[:, 5, :]
                    mul = nc.vector.tensor_tensor(cen[:, :, :], z, h, ALU.mult)
                    steps.then(mul)
                    steps.then(nc.vector.reduce_sum(dot, cen[:, :, :], AX))
                    steps.then(nc.vector.tensor_scalar(dot, dot, -R_CONST, F_CONST, ALU.mult,
                                                       ALU.add))
                    steps.then(nc.vector.scalar_tensor_tensor(out=cen2[:, :, :], in0=h,
                                                              scalar=-B_CONST, in1=spread(dot),
                                                              op0=ALU.mult, op1=ALU.add))
                    steps.then(nc.vector.tensor_tensor(new_x[:, :, :], x_i, cen2[:, :, :], ALU.add))
                    norm(steps, new_x[:, :, :], v_next)
                    keep(x_i)
                elif k in (4, 5):
                    b = bias_sb[:, k - 4:k - 3, :].broadcast_to([P, NT, D])
                    add = nc.vector.tensor_tensor(v_next, z, b, ALU.add)
                    add.then_inc(vec_ready, 1)
                elif k == 6:
                    b = bias_sb[:, 2:3, :].broadcast_to([P, NT, D])
                    add = nc.vector.tensor_tensor(cen[:, :, :], z, b, ALU.add)
                    steps.then(add)
                    steps.then(nc.vector.tensor_tensor(new_x[:, :, :], x_i, cen[:, :, :], ALU.add))
                    norm(steps, new_x[:, :, :], v_next, scale=dinv[:, tiles])
                    keep(x_i)
                elif k == 7:
                    mul = nc.vector.tensor_tensor(cen[:, :, :], z, spread(dinv[:, tiles]), ALU.mult)
                    steps.then(mul)
                    nc.vector.tensor_tensor(result[:, tiles, :], x_i, cen[:, :, :],
                                            ALU.add).then_inc(vec_ready, 1)
                assert k == 1 or steps.n == POST_STEPS[k], (k, steps.n)

            def copy_alone(k, s):
                alone_banks = alone_ps[:, :, :].rearrange("p b i -> p (b i)")
                fin, beg, cols = parts(k, s)
                after(dve, post_done, strips_before(k, s))
                dve.wait_ge(alone_done, strips_before(k, s) + 1)
                if k in TURNED:
                    nc.vector.tensor_copy(alone_sb[:, :], alone_banks).then_inc(alone_copied, 1)
                    return
                first = nc.vector.tensor_tensor(alone_sb[fin, :], alone_banks[fin],
                                                partial[fin, cols], ALU.add)
                if is_first(s):
                    first.then_inc(shared_copied, 1)
                nc.vector.tensor_copy(alone_sb[beg, :], alone_banks[beg]).then_inc(alone_copied, 1)

            def parts(k, s):
                fin, beg = D * ((k - 1) % 2), D * (k % 2)
                cols = bass.ds(strip_of(k, s) * SW, SW)
                fin, beg = slice(fin, fin + D), slice(beg, beg + D)
                computed(dve, partial[fin, cols], partial[beg, cols])
                return fin, beg, cols

            def copy_shared(k, s):
                fin, beg, cols = parts(k, s)
                banks = shared_ps[:, :, :].rearrange("p b i -> p (b i)")
                if is_first(s) or k == SWEEPS:
                    if k in TURNED:
                        if k > 1:
                            apart(dve)
                        after(dve, post_done, strips_before(k, s))
                        if k == 1:
                            nc.vector.memset(shared_sb[fin, :], 0.0).then_inc(shared_copied, 1)
                        else:
                            nc.vector.tensor_copy(shared_sb[fin, :], partial[fin, cols]).then_inc(
                                shared_copied, 1)
                    if k < SWEEPS:
                        nc.vector.memset(partial[beg, cols], 0.0).then_inc(partial_kept, 1)
                    return
                if k not in TURNED:
                    dve.wait_ge(alone_copied, strips_before(k, s) + 1)
                dve.wait_ge(shared_done, (T - 1) * (k - 1) + s)
                if k == 1:
                    nc.vector.tensor_copy(shared_sb[fin, :], banks[fin]).then_inc(shared_copied, 1)
                elif k == 2:
                    nc.vector.tensor_tensor(shared_sb[fin, :], banks[fin], partial[fin, cols],
                                            ALU.add).then_inc(shared_copied, 1)
                else:
                    nc.vector.tensor_tensor(alone_sb[fin, :], banks[fin], alone_sb[fin, :],
                                            ALU.add).then_inc(shared_copied, 1)
                nc.vector.tensor_copy(partial[beg, cols], banks[beg]).then_inc(partial_kept, 1)

            def add_rows(src, landed, landings, n, begins=False):
                for q in range(NQ):
                    dve.wait_ge(landed[q], landings)
                    if begins and q == 0:
                        nc.vector.tensor_copy(row_sums, src[:, q]).then_inc(rows_added, 1)
                        continue
                    dve.wait_ge(rows_added, NQ * n + q)
                    nc.vector.tensor_tensor(row_sums, row_sums, src[:, q], ALU.add).then_inc(
                        rows_added, 1)

            def copy_degrees(s):
                dve.wait_ge(deg_done, s + 1)
                nc.vector.tensor_copy(degree[:, bass.ds(s * NT, NT)], deg_ps[:, 0:NT]).then_inc(
                    deg_copied, 1)

            def inverse_roots():
                steps = Steps(steps_used[0])
                deg, floor, y, t = (dtmp[:, c, :] for c in range(4))
                dve.wait_ge(deg_copied, STARTED + T)
                steps.then(nc.vector.tensor_scalar(deg, degree[:, :], 1.0, None, ALU.add))
                steps.then(nc.vector.tensor_scalar(floor, deg, TINY, None, ALU.max))
                rsqrt(steps, y, floor, t)
                steps.then(nc.vector.scalar_tensor_tensor(out=dinv[:, :], in0=deg, scalar=0.0, in1=y,
                                                          op0=ALU.is_gt, op1=ALU.mult))
                steps_used[0] += steps.n

            def first_norm(n, c):
                tiles = slice(c * NT, (c + 1) * NT)
                if n < 2:
                    dve.wait_ge(x_loaded[n], 16 if n == 0 else 16 * (T - 1))
                if n:
                    dve.wait_ge(vec_ready, n)
                steps = Steps(steps_used[0])
                norm(steps, resid[:, tiles, :], vecs[:, tiles, 0, :])
                steps_used[0] += steps.n

            def strip(k, s, early=False):
                if k == 1:
                    if not is_first(s):
                        copy_degrees(s - 1)
                    add_rows(diag, diag_landed, 16 * (s + 1), T * s, begins=True)
                    if is_first(s):
                        for a, c in enumerate(FIRST_USED[1:]):
                            first_norm(a + 1, c)
                            add_rows(tri, tri_landed, 16 * (a + 1), 1 + a)
                        copy_shared(k, s)
                        copy_alone(k, s)
                        return

                    def add(place, n_tri, _):
                        add_rows(tri, tri_landed, 16 * (n_tri + 1), place)

                    sweep_one(dve, s, early, add, add, lambda: None, lambda: copy_alone(k, s))
                    copy_shared(k, s)
                    return
                if not is_first(s):
                    post(k, s - 1)
                if is_first(s) or k == SWEEPS:
                    copy_shared(k, s)
                    copy_alone(k, s)
                else:
                    copy_alone(k, s)
                    copy_shared(k, s)
                if k == 2 and is_first(s):
                    copy_degrees(T - 1)
                    inverse_roots()

            first_norm(0, 0)
            dve.wait_ge(w_loaded, 16 * 5)
            for k in range(1, SWEEPS + 1):
                if k > 1:
                    dve.wait_ge(partial_kept, T * (k - 1))
                over_strips(dve, k, strip)
                if k > 1:
                    post(k, T - 1)
                    steps_used[0] += POST_STEPS[k] * T


def kernel(x, adj, L0_gnn_W, L1_gnn_t, L2_gnn_W0, L2_gnn_b0, L2_gnn_W1, L2_gnn_b1, L2_gnn_W2,
           L2_gnn_b2, L3_gnn_W):
    import numpy as np
    import concourse.bacc as bacc
    from concourse import mybir as mb
    from concourse.bass_utils import run_bass_kernel_spmd

    n = x.shape[0]
    t = n // SW
    a = {}
    a["x_rows"] = np.ascontiguousarray(np.asarray(x).reshape(n // P, P, D).transpose(1, 0, 2))
    a["adj_units"] = np.ascontiguousarray(
        np.asarray(adj).reshape(t, SW, t, NQ, 2, P).transpose(0, 2, 3, 5, 4, 1)).reshape(
            t * t * NQ, P, 2 * SW)
    w0 = np.asarray(L0_gnn_W)
    eye = np.eye(P, dtype=np.float32)
    a["w_right"] = np.stack([w0[0, :D], w0[1, :D], eye[:D, :D], np.asarray(L2_gnn_W0).T,
                             np.asarray(L2_gnn_W1).T, np.asarray(L2_gnn_W2).T, np.asarray(L3_gnn_W)])
    a["w_concat"] = np.stack([w0[0], np.concatenate([w0[1, D:], w0[1, :D]])])
    a["bias_rows"] = np.ascontiguousarray(np.broadcast_to(
        np.stack([np.asarray(b) for b in (L2_gnn_b0, L2_gnn_b1, L2_gnn_b2)]), (P, 3, D)))
    a["eye"] = eye
    nc = bacc.Bacc("TRN2", target_bir_lowering=False, num_devices=1)
    aps = [nc.dram_tensor(name, v.shape, mb.dt.float32, kind="ExternalInput").ap()
           for name, v in a.items()]
    out = nc.dram_tensor("out_rows", a["x_rows"].shape, mb.dt.float32, kind="ExternalOutput").ap()
    graph_layers(nc, *aps, out)
    r = run_bass_kernel_spmd(nc, [a], core_ids=[0])
    rows = r.results[0]["out_rows"]
    return np.ascontiguousarray(rows.transpose(1, 0, 2)).reshape(n, D)
```

```python
from contextlib import ExitStack

import concourse.bass as bass
from concourse import mybir

F32 = mybir.dt.float32
I32 = mybir.dt.int32
ALU = mybir.AluOpType
ACT = mybir.ActivationFunctionType
AX = mybir.AxisListType.X

P = 128
D = 64
SW = 1024
NT = SW // P
NQ = 4
BANK = 512
NI = SW // BANK
SWEEPS = 7
EPS = 1e-5
F_CONST, B_CONST, R_CONST = 1.0, 0.1, 0.01
TINY = 1.1754944e-38
RSQRT_GUESS = float(0x5F3759DF)
TURNED = (1, 2, 7)
BY_SQUARE = (4, 5, 6)


def graph_layers(nc, x, adj, wstack, wcat, bias, eye, out):
    NTILES = x.shape[1]
    T = NTILES // NT
    assert adj.shape[0] == T * T * NQ and T >= 4 and T % 2 == 0
    TRI = T * (T - 1) // 2
    FIRST_USED = list(range(T - 1, -1, -1))

    def strip_of(k, s):
        return s if k % 2 else (T - 1) - s

    def tri_index(k, s, u):
        return (k - 1) * TRI + s * (s - 1) // 2 + u

    def right_index(s, a):
        before = (2 * T - 1 - s) * s // 2
        if not isinstance(s, int):
            before = before & 0xFFFF
        return before + a

    def place(k, s, u):
        base = T * (T + 1) + (k - 2) * (TRI + T)
        return base + (s * (s - 1) // 2 if k == SWEEPS else (s - 1) * (s + 2) // 2) + u

    def diag_place(k, d):
        if isinstance(d, int) and d >= T - 2:
            return T * (T + 1) + (k - 2) * (TRI + T) + TRI + d
        return place(k, d + 2, 0) - 1

    def square_place(k, s, u):
        base = (k - 3) * (TRI + T)
        return base + (s * (s - 1) // 2 if k == 6 else (s - 1) * (s + 2) // 2) + u

    def diag_square_place(k, d):
        if isinstance(d, int) and d >= T - 2:
            return (k - 3) * (TRI + T) + TRI + d
        return square_place(k, d + 2, 0) - 1

    def diags_used(k, d):
        return T * k + d

    def diags_landed(k, d):
        return T + (T - 1) * (k - 2) + d

    def early_pair_index(s, b):
        return ((((2 * T - 5 - s) * s + 2 * (T - 1)) // 2) & 0xFFFF) + b

    def late_rest_index(s, c):
        return (((s * (s - 3) + 2 * (T - 1)) // 2) & 0xFFFF) + c

    def folds_before(k, d):
        return T * (k - 1) + d

    def strips_before(k, s):
        return T * (k - 1) + s

    def over_strips(eng, k, strip, peeled=2):
        if k > 1:
            for s in range(peeled):
                strip(k, s)
            with eng.Fori(peeled, T) as s:
                strip(k, s)
            return
        strip(k, 0)
        with eng.Fori(1, T // 2) as s:
            strip(k, s, early=True)
        with eng.Fori(T // 2, T - 1) as s:
            strip(k, s)
        strip(k, T - 1)

    def sweep_one(eng, s, early, alone, shared, next_diag, own_diag):
        if is_first(s):
            with eng.Fori(0, T - 1) as a:
                alone(a, a, a, 1, (T - 1) - a)
            own_diag(T - 1, T - 1)
            return
        if early:
            with eng.Fori(0, T - 1 - 2 * s) as a:
                alone((T + 1) * s - 1 + a, right_index(s, a), T * s + a, 1, (T - 1) - a)
            next_diag((T - 1) * s + (T - 2))
            with eng.Fori(0, s) as b:
                shared((T - 1) * s + (T - 1) + 2 * b, tri_index(1, s, b),
                       (T - 2) * s + (T - 1) + 2 * b, 2, b, b + 1)
                alone((T - 1) * s + T + 2 * b, early_pair_index(s, b),
                      (T - 2) * s + T + 2 * b, 2, 2 * s - b)
        elif is_last(s):
            at = (T + 1) * s - 1
            with eng.Fori(0, T // 2) as b:
                shared(at + b, tri_index(1, s, b), T * s + b, 1, b, b + 1)
            next_diag(at + T // 2)
            with eng.Fori(T // 2, s) as b:
                shared(at + 1 + b, tri_index(1, s, b), T * s + b, 1, b, b + 1)
        else:
            with eng.Fori(0, T - 1 - s) as b:
                alone((T + 1) * s - 1 + 2 * b, right_index(s, b), T * s + 2 * b, 2, (T - 1) - b)
                shared((T + 1) * s + 2 * b, tri_index(1, s, b), T * s + 1 + 2 * b, 2, b, b + 1)
            next_diag((T - 1) * s + (2 * T - 3))
            with eng.Fori(0, 2 * s - (T - 1)) as c:
                shared((T - 1) * s + (2 * T - 2) + c, late_rest_index(s, c),
                       (T - 2) * s + (2 * T - 2) + c, 1, (T - 1) - s + c, s)
        own_diag((T + 1) * s + (T - 1), T * s + (T - 1))

    def is_first(s):
        return isinstance(s, int) and s == 0

    def is_last(s):
        return isinstance(s, int) and s == T - 1

    with ExitStack() as ctx:
        def sb(name, shape, dt=F32):
            return ctx.enter_context(nc.sbuf_tensor(name, shape, dt))

        def ps(name, shape):
            return ctx.enter_context(nc.psum_tensor(name, shape, F32))

        def sem(name):
            return ctx.enter_context(nc.semaphore(name))

        diag = sb("diag", [P, NQ, 2, SW])
        tri = sb("tri", [P, NQ, 2, SW])
        sq = sb("sq", [P, NQ, 2, SW])
        right = sq
        result = sq[:, :, :, :].rearrange("p q b i -> p (q b i)")[:, 0:T * NT * D].rearrange(
            "p (t d) -> p t d", d=D)
        vecs = sb("vecs", [P, NTILES, 2, D])
        resid = sb("resid", [P, NTILES, D])
        partial = sb("partial", [P, NTILES * P])
        stage = sb("stage", [P, 2, NT // 2, 2, D])
        scratch = sb("scratch", [P, 2, SW])
        row_sums = scratch[:, :, :]
        own_sb = sb("own_sb", [P, NT, D])
        sum_sb = sb("sum_sb", [P, SW])
        alone_moved = sb("alone_moved", [P, BANK])
        next_moved = sb("next_moved", [P, BANK])
        cen, cen2, new_x = (scratch[:, c // 2, c % 2 * BANK:(c % 2 + 1) * BANK].rearrange(
            "p (t d) -> p t d", d=D) for c in range(3))
        small = sb("small", [P, 6, NT])
        degree = sb("degree", [P, NTILES])
        dinv = sb("dinv", [P, NTILES])
        dtmp = sb("dtmp", [P, 4, NTILES])
        x_sum, x_dev, neg_mean, x_scale = (dtmp[:, c, :] for c in range(4))
        x_shift = dinv
        w_top = sb("w_top", [P, SWEEPS, D])
        w_cat = sb("w_cat", [P, len(TURNED), D])
        bias_sb = sb("bias_sb", [P, 3, D])
        ident = sb("ident", [P, P])
        zeros = sb("zeros", [P, P], mybir.dt.bfloat16)
        ones = sb("ones", [P, 2])
        nil = sb("nil", [P, 1])

        alone_ps = ps("alone_ps", [P, BANK])
        next_ps = ps("next_ps", [P, BANK])
        shared_ps = ps("shared_ps", [P, NI, BANK])
        turn_ps = ps("turn_ps", [P, NI, BANK])
        post_ps = ps("post_ps", [P, BANK])
        deg_ps = ps("deg_ps", [P, BANK])

        x_loaded = [sem("x_loaded_first"), sem("x_loaded_second"), sem("x_loaded_rest")]
        w_loaded = sem("w_loaded")
        consts_set = sem("consts_set")
        diag_landed = [sem(f"diag_landed{q}") for q in range(NQ)]
        tri_landed = [sem(f"tri_landed{q}") for q in range(NQ)]
        right_landed = [sem(f"right_landed{q}") for q in range(NQ)]
        right_used = [sem(f"right_used{q}") for q in range(NQ)]
        diag_used = [sem(f"diag_used{q}") for q in range(NQ)]
        tri_used = [sem(f"tri_used{q}") for q in range(NQ)]
        sq_ready = [sem(f"sq_ready{q}") for q in range(NQ)]
        sq_free = [sem(f"sq_free{q}") for q in range(NQ)]
        stage_ready = [sem(f"stage_ready{j}") for j in range(2)]
        stage_free = [sem(f"stage_free{j}") for j in range(2)]
        vec_ready = sem("vec_ready")
        vec_begun = sem("vec_begun")
        x_summed = sem("x_summed")
        mean_ready = sem("mean_ready")
        x_squared = sem("x_squared")
        scale_ready = sem("scale_ready")
        own_ready = sem("own_ready")
        rows_cleared = sem("rows_cleared")
        rows_added = sem("rows_added")
        rows_folded = sem("rows_folded")
        deg_done = sem("deg_done")
        deg_copied = sem("deg_copied")
        alone_done = sem("alone_done")
        alone_split = sem("alone_split")
        next_done = sem("next_done")
        next_split = sem("next_split")
        folded = sem("folded")
        shared_done = sem("shared_done")
        sum_begun = sem("sum_begun")
        sum_ready = sem("sum_ready")
        partial_kept = sem("partial_kept")
        turned = sem("turned")
        turn_copied = sem("turn_copied")
        post_done = sem("post_done")
        tanh_ready = sem("tanh_ready")
        resid_kept = sem("resid_kept")
        STARTED = 1
        started = [deg_copied, resid_kept, folded, *sq_free]
        step = sem("step")
        out_stored = sem("out_stored")

        turns_before = {1: 0, 2: T, 7: 2 * T}

        def computed(eng, *values):
            for v in values:
                if isinstance(v, bass.AP):
                    (eng.lower_ap_dma if v.tensor.name == adj.tensor.name else eng.lower_ap)(v)
                elif not isinstance(v, int):
                    eng.compute_val(v)

        def after(eng, sem, count):
            if not (isinstance(count, int) and count <= 0):
                eng.wait_ge(sem, count)

        def apart(eng):
            eng.wait_ge(consts_set, 1)

        block = ctx.enter_context(nc.Block())

        @block.sync
        def _(sp):
            first = slice(FIRST_USED[0] * NT, (FIRST_USED[0] + 1) * NT)
            sp.dma_start(resid[:, first, :], x[:, first, :]).then_inc(x_loaded[0], 16)

            def load_d(i, used, row):
                first = i * (T + 1) * NQ
                for q in range(NQ):
                    if row is not None:
                        computed(sp, NQ * (row - T) + q + 1)
                    computed(sp, adj[first + q], used)
                    if row is not None:
                        sp.wait_ge(rows_added, NQ * (row - T) + q + 1)
                    after(sp, diag_used[q], used)
                    sp.dma_start(diag[:, q].rearrange("p b i -> p (b i)"), adj[first + q]).then_inc(
                        diag_landed[q], 16)

            def load_t(i, j, n, row, lag=0, slots=tri, landed=tri_landed, used=tri_used):
                first = (i * T + j) * NQ
                for q in range(NQ):
                    computed(sp, adj[first + q], n)
                    if row is not None:
                        sp.wait_ge(rows_added, NQ * (row - lag) + q + 1)
                    after(sp, used[q], n)
                    sp.dma_start(slots[:, q].rearrange("p b i -> p (b i)"), adj[first + q]).then_inc(
                        landed[q], 16)

            def strip(k, s, early=False):
                i = strip_of(k, s)
                if k == 1:
                    def load_right(_, n, row, lag, j):
                        load_t(i, j, n, row, lag, right, right_landed, right_used)

                    if is_first(s):
                        for a in range(T - 1):
                            load_right(None, a, a if a else None, 1, (T - 1) - a)
                        load_d(i, 0, None)
                        return
                    sweep_one(sp, s, early, load_right,
                              lambda _, n, row, lag, j, strips: load_t(i, j, n, row, lag),
                              lambda _: None, lambda _, row: load_d(i, 2 * s, row))
                elif not is_first(s):
                    if k < SWEEPS and not (isinstance(s, int) and s < 3):
                        load_d(strip_of(k, s - 2), diags_used(k, s - 2), None)
                    with sp.Fori(0, s) as u:
                        load_t(i, strip_of(k, u), tri_index(k, s, u), None)

            for k in range(1, SWEEPS + 1):
                if k == 2:
                    sp.wait_ge(rows_added, NQ * T * T)
                over_strips(sp, k, strip, peeled=3)
                if 1 < k < SWEEPS:
                    for d in (T - 2, T - 1):
                        load_d(strip_of(k, d), diags_used(k, d), None)

        @block.gpsimd
        def _(pool):
            for c, count in enumerate(started):
                nc.gpsimd.memset(zeros[:, c * 16:(c + 1) * 16], 0.0).then_inc(count, STARTED)
            nc.gpsimd.memset(zeros[:, len(started) * 16:], 0.0)
            nc.gpsimd.memset(nil[:, :], 0.0)
            nc.gpsimd.memset(ones[:, :], 1.0).then_inc(consts_set, 1)

            def put_own(k, s):
                v = vecs[:, bass.ds(strip_of(k, s) * NT, NT), (k - 1) % 2, :]
                computed(pool, v, turns_before[k] + s)
                apart(pool)
                after(pool, turned, turns_before[k] + s)
                nc.gpsimd.tensor_copy(own_sb[:, :, :], v).then_inc(own_ready, 1)

            def put(j, n, half, strips=None, of_h=False):
                for h in range(2):
                    tiles = bass.ds(j * NT + h * (NT // 2), NT // 2)
                    wanted = None if strips is None or (h == 1 and of_h) else (
                        (vec_begun, strips - T) if h == 0 and not of_h else (vec_ready, strips))
                    computed(pool, n, *([] if wanted is None else [wanted[1]]),
                             vecs[:, tiles, 0 if half is None else half, :])
                    apart(pool)
                    after(pool, stage_free[h], n)
                    if wanted is not None:
                        pool.wait_ge(*wanted)
                    if half is None:
                        nc.gpsimd.tensor_copy(stage[:, h], vecs[:, tiles, :, :]).then_inc(
                            stage_ready[h], 1)
                    else:
                        nc.gpsimd.tensor_copy(stage[:, h, :, half, :],
                                              vecs[:, tiles, half, :]).then_inc(stage_ready[h], 1)

            def strip(k, s, early=False):
                f = (k - 1) % 2
                if k == 1:
                    if not is_first(s):
                        put_own(k, s)

                    def own_diag(n, _):
                        put(s, n, 0, strips=T if is_first(s) else None, of_h=True)
                        if is_first(s):
                            put_own(k, s)

                    sweep_one(pool, s, early,
                              lambda n, _, row, lag, j: put(
                                  j, n, 0, strips=n + 1 if is_first(s) else None, of_h=True),
                              lambda n, _, row, lag, j, strips: put(j, n, None, strips=T + strips),
                              lambda n: put(s - 1, n, 1, strips=T + s), own_diag)
                    return
                if is_first(s):
                    pool.wait_ge(vec_ready, T * k)
                if k in TURNED:
                    put_own(k, s)
                if is_first(s):
                    return
                if k < SWEEPS and not (isinstance(s, int) and s == 1):
                    put(strip_of(k, s - 2), diag_place(k, s - 2), k % 2, strips=T * k + s - 1)
                with pool.Fori(0, s) as u:
                    if k < SWEEPS:
                        put(strip_of(k, u), place(k, s, u), None, strips=T * k + u + 1)
                    else:
                        put(strip_of(k, u), place(k, s, u), f)

            for k in range(1, SWEEPS + 1):
                over_strips(pool, k, strip)
                if k == 1:
                    put(T - 1, T * (T + 1) - 1, 1, strips=2 * T)
                elif k < SWEEPS:
                    for d in (T - 2, T - 1):
                        put(strip_of(k, d), diag_place(k, d), k % 2, strips=T * k + d + 1)

        @block.scalar
        def _(act):
            for n, (lo, hi) in enumerate(((T - 2, T - 1), (0, T - 2))):
                act.dma_start(resid[:, lo * NT:hi * NT, :], x[:, lo * NT:hi * NT, :]).then_inc(
                    x_loaded[n + 1], 16)

            def load_constants():
                act.dma_start(ident[:, :], eye).then_inc(w_loaded, 16)
                act.dma_start(w_cat[:, :, :], wcat.rearrange("k a b -> a k b")).then_inc(w_loaded, 16)
                for h in range(2):
                    act.dma_start(w_top[h * D:(h + 1) * D],
                                  wstack.rearrange("k a b -> a k b")).then_inc(w_loaded, 16)
                act.dma_start(bias_sb[:, :, :], bias).then_inc(w_loaded, 16)

            act.wait_ge(consts_set, 1)

            def clear_rows(s):
                for b, (read, count) in ((1, (rows_folded, s)), (0, (deg_done, s))):
                    after(act, read, count)
                    nc.scalar.activation(row_sums[:, b], nil[:, 0:1].broadcast_to([P, SW]),
                                         ACT.Copy).then_inc(rows_cleared, 1)

            def copy_begun(s):
                kept = partial[D:P, bass.ds(s * SW, SW)]
                banks = shared_ps[:, :, :].rearrange("p b i -> p (b i)")
                computed(act, kept)
                act.wait_ge(shared_done, s)
                act.wait_ge(post_done, s)
                nc.scalar.activation(sum_sb[0:D, :], banks[0:D], ACT.Copy).then_inc(sum_begun, 1)
                nc.scalar.activation(kept, banks[D:P], ACT.Copy).then_inc(partial_kept, 1)

            unused = tri[:, :, :, :].rearrange("p q b i -> p (q b i)")

            def by_tile(n, func, done, out, **how):
                for t in range(FIRST_USED[n] * NT, (FIRST_USED[n] + 1) * NT):
                    col = {name: v[:, t:t + 1] for name, v in how.items()}
                    last = nc.scalar.activation(out(t), resid[:, t, :], func, **col)
                last.then_inc(done, 1)

            def add_up(n):
                if n < 3:
                    act.wait_ge(x_loaded[n], 16)
                by_tile(n, ACT.Copy, x_summed, lambda t: unused[:, t * P:t * P + D],
                        accum_out=x_sum)

            add_up(1)
            for n in range(1, T):
                if n + 1 < T:
                    add_up(n + 1)
                act.wait_ge(mean_ready, n)
                by_tile(n, ACT.Square, x_squared, lambda t: unused[:, t * P + D:(t + 1) * P],
                        bias=neg_mean, accum_out=x_dev)
                if n == 1:
                    clear_rows(0)
                act.wait_ge(scale_ready, n)
                by_tile(n, ACT.Relu, vec_ready, lambda t: vecs[:, t, 0, :], bias=x_shift,
                        scale=x_scale)
                if n == 1:
                    load_constants()

            def square(q, src, landed, landings, m, squared):
                act.wait_ge(landed[q], landings)
                act.wait_ge(sq_free[q], STARTED + m)
                nc.scalar.activation(sq[:, q], src[:, q], ACT.Square).then_inc(squared[q], 1)

            def post(k, s):
                i = strip_of(k, s)
                act.wait_ge(post_done, strips_before(k, s) + 1)
                z = post_ps[:, :].rearrange("p (t d) -> p t d", d=D)
                if k == 2:
                    act.wait_ge(resid_kept, STARTED + s)
                for h in range(2):
                    half = slice(h * NT // 2, (h + 1) * NT // 2)
                    if k == 1:
                        nc.scalar.activation(vecs[:, bass.ds(i * NT + h * NT // 2, NT // 2), 1, :],
                                             z[:, half], ACT.Tanh).then_inc(
                                                 vec_ready if h else vec_begun, 1)
                    else:
                        nc.scalar.activation(new_x[:, half, :], z[:, half], ACT.Tanh).then_inc(
                            tanh_ready, 1)

            def copy_turned(k, s):
                other = D * (k % 2)
                act.wait_ge(turned, turns_before[k] + s + 1)
                after(act, post_done, strips_before(k, s))
                nc.scalar.activation(sum_sb[other:other + D, :],
                                     turn_ps[other:other + D].rearrange("p b i -> p (b i)"),
                                     ACT.Copy).then_inc(turn_copied, 1)

            def square_diag(k, d):
                for q in range(NQ):
                    square(q, diag, diag_landed, 16 * diags_landed(k, d), diag_square_place(k, d),
                           diag_used)

            def strip(k, s, early=False):
                if k == 1 and not is_first(s):
                    clear_rows(s)
                if k in TURNED:
                    if k < SWEEPS and not is_first(s):
                        post(k, s - 1)
                    copy_turned(k, s)
                    if k == 1 and not is_first(s):
                        copy_begun(s)
                if 3 <= k <= 5 and not is_first(s) and not (isinstance(s, int) and s == 1):
                    square_diag(k, s - 2)
                if 3 <= k <= 6 and not is_first(s):
                    with act.Fori(0, s) as u:
                        for q in range(NQ):
                            square(q, tri, tri_landed, 16 * (tri_index(k, s, u) + 1),
                                   square_place(k, s, u), tri_used if k in (4, 5) else sq_ready)
                if k == SWEEPS and not is_first(s):
                    store(s - 1)

            def store(s):
                act.wait_ge(vec_ready, strips_before(SWEEPS + 1, s) + 1)
                tiles = bass.ds(strip_of(SWEEPS, s) * NT, NT)
                act.dma_start(out[:, tiles, :], result[:, tiles, :]).then_inc(out_stored, 16)

            for k in range(1, SWEEPS + 1):
                if k == 3:
                    for q in range(NQ):
                        act.wait_ge(right_used[q], TRI)
                    act.wait_ge(rows_added, NQ * T * T)
                over_strips(act, k, strip)
                if k < 3:
                    post(k, T - 1)
                if 3 <= k <= 5:
                    square_diag(k, T - 2)
                    square_diag(k, T - 1)
            store(T - 1)
            act.wait_ge(out_stored, 16 * T)

        @block.tensor
        def _(pe):
            def add_zero(bank, cols, **flags):
                return nc.tensor.matmul(bank[0:cols, 0:1], zeros[:, 0:cols], zeros[:, 0:1],
                                        skip_group_check=True, **flags)

            def alone(bank, half, src, n, ready, value, freed):
                computed(pe, n + 1, value)
                for q in range(NQ):
                    h = q // 2
                    if q % 2 == 0:
                        pe.wait_ge(stage_ready[h], n + 1)
                    pe.wait_ge(ready[q], value)
                    for b in range(2):
                        for i in range(NI):
                            last = nc.tensor.matmul(
                                bank[i * D:(i + 1) * D, :], stage[:, h, 2 * (q % 2) + b, half, :],
                                src[:, q, b, i * BANK:(i + 1) * BANK],
                                start=False, stop=False, skip_group_check=True)
                            if q == 2 and b == 0 and i == 0:
                                last.then_inc(stage_free[0], 1)
                    last.then_inc(freed[q], 1)
                add_zero(bank, D, start=False, stop=False).then_inc(stage_free[1], 1)

            def next_alone(k, d, n):
                pe.wait_ge(folded, STARTED + folds_before(k, d))
                bounds([next_ps], True)
                if k == 1:
                    alone(next_ps, 1, diag, n, diag_landed, 16 * (d + 1), diag_used)
                elif k + 1 in BY_SQUARE:
                    alone(next_ps, k % 2, sq, n, diag_used, diags_used(k, d) + 1, sq_free)
                else:
                    alone(next_ps, k % 2, diag, n, diag_landed, 16 * diags_landed(k, d), diag_used)
                bounds([next_ps], False).then_inc(next_done, 1)

            def turn(k, s):
                other = D * (k % 2)
                if k == 1 and is_first(s):
                    pe.wait_ge(w_loaded, 16 * 5)
                pe.wait_ge(own_ready, turns_before[k] + s + 1)
                after(pe, turn_copied, turns_before[k] + s)
                for t in range(NT):
                    h, c = divmod(t, NT // 2)
                    last = nc.tensor.matmul(turn_ps[other:other + D, h, c * P:(c + 1) * P],
                                            own_sb[:, t, :], ident[:, :], start=True, stop=True)
                last.then_inc(turned, 1)

            def shared(k, n, n_tri, m):
                computed(pe, n + 1, 16 * (n_tri + 1))
                for q in range(NQ):
                    h = q // 2
                    if q % 2 == 0:
                        pe.wait_ge(stage_ready[h], n + 1)
                    if k in (1, 2, 3, 6):
                        pe.wait_ge(tri_landed[q], 16 * (n_tri + 1))
                    if k in (3, 6):
                        pe.wait_ge(sq_ready[q], m + 1)
                    if k in (4, 5):
                        pe.wait_ge(tri_used[q], n_tri + 1)
                    for b in range(2):
                        both = stage[:, h, 2 * (q % 2) + b].rearrange("p g d -> p (g d)")
                        for i in range(NI):
                            cols = slice(i * BANK, (i + 1) * BANK)
                            ends = b == 1 and i == NI - 1
                            if k in (3, 6):
                                of_a, of_w = [nc.tensor.matmul(
                                    shared_ps[g * D:(g + 1) * D, i, :], both[:, g * D:(g + 1) * D],
                                    src[:, q, b, cols], start=False, stop=False,
                                    skip_group_check=True) for g, src in enumerate((tri, sq))]
                                first = of_a
                                if ends:
                                    of_a.then_inc(tri_used[q], 1)
                                    of_w.then_inc(sq_free[q], 1)
                            else:
                                src, used = (tri, tri_used) if k < 3 else (sq, sq_free)
                                first = nc.tensor.matmul(shared_ps[:, i, :], both,
                                                         src[:, q, b, cols], start=False,
                                                         stop=False, skip_group_check=True)
                                if ends:
                                    first.then_inc(used[q], 1)
                            if q == 2 and b == 0 and i == 0:
                                first.then_inc(stage_free[0], 1)
                add_zero(shared_ps[:, 0], P, start=False, stop=False).then_inc(stage_free[1], 1)

            def bounds(banks, opens):
                for bank in banks:
                    last = add_zero(bank, P, start=opens, stop=not opens)
                return last

            def post(k, s):
                before = strips_before(k, s)
                f = (k - 1) % 2
                pe.wait_ge(sum_ready, before + 1)
                if k in TURNED:
                    pe.wait_ge(turn_copied, turns_before[k] + s + 1)
                pe.wait_ge(vec_ready, T + before)
                rows, w = ((slice(0, P), w_cat[:, TURNED.index(k), :]) if k in TURNED else
                           (slice(f * D, (f + 1) * D), w_top[f * D:(f + 1) * D, k - 1, :]))
                for t in range(NT):
                    last = nc.tensor.matmul(post_ps[:, t * D:(t + 1) * D],
                                            sum_sb[rows, t * P:(t + 1) * P], w,
                                            start=True, stop=True)
                last.then_inc(post_done, 1)

            def sum_degrees(s):
                pe.wait_ge(rows_folded, s + 1)
                pe.wait_ge(deg_copied, STARTED + s)
                for t in range(NT):
                    last = nc.tensor.matmul(deg_ps[:, t:t + 1], row_sums[:, 0, t * P:(t + 1) * P],
                                            ones[:, 0:1], start=True, stop=True)
                last.then_inc(deg_done, 1)

            shared_banks = [shared_ps[:, i] for i in range(NI)]

            def open_alone(k, s):
                after(pe, sum_ready, strips_before(k, s))
                bounds([alone_ps], True)

            def open_shared(k, s):
                pe.wait_ge(partial_kept, strips_before(k, s))
                bounds(shared_banks, True)

            def strip(k, s, early=False):
                if k == 1:
                    if not is_first(s):
                        sum_degrees(s - 1)
                        post(k, s - 1)
                        turn(k, s)
                        open_shared(k, s)
                    open_alone(k, s)

                    def own_diag(n, _):
                        if is_first(s):
                            turn(k, s)
                        else:
                            bounds(shared_banks, False).then_inc(shared_done, 1)
                        alone(alone_ps, 0, diag, n, diag_landed, 16 * (s + 1), diag_used)
                        bounds([alone_ps], False).then_inc(alone_done, 1)

                    sweep_one(pe, s, early,
                              lambda n, n_right, *_: alone(alone_ps, 0, right, n, right_landed,
                                                           16 * (n_right + 1), right_used),
                              lambda n, n_tri, *_: shared(k, n, n_tri, None),
                              lambda n: next_alone(k, s - 1, n), own_diag)
                    return
                if k < SWEEPS and not is_first(s) and not (isinstance(s, int) and s == 1):
                    next_alone(k, s - 2, diag_place(k, s - 2))
                if not is_first(s):
                    post(k, s - 1)
                if k in TURNED:
                    turn(k, s)
                if is_first(s):
                    return
                if k < SWEEPS:
                    open_shared(k, s)
                    with pe.Fori(0, s) as u:
                        m = (0 if k == 3 else TRI) + s * (s - 1) // 2 + u
                        shared(k, place(k, s, u), tri_index(k, s, u), m)
                    bounds(shared_banks, False).then_inc(shared_done, 1)
                else:
                    open_alone(k, s)
                    with pe.Fori(0, s) as u:
                        alone(alone_ps, 0, tri, place(k, s, u), tri_landed,
                              16 * (tri_index(k, s, u) + 1), tri_used)
                    bounds([alone_ps], False).then_inc(alone_done, 1)

            pe.wait_ge(consts_set, 1)
            for k in range(1, SWEEPS + 1):
                over_strips(pe, k, strip)
                post(k, T - 1)
                if k == 1:
                    sum_degrees(T - 1)
                    next_alone(k, T - 1, T * (T + 1) - 1)
                elif k < SWEEPS:
                    for d in (T - 2, T - 1):
                        next_alone(k, d, diag_place(k, d))

        @block.vector
        def _(dve):
            class Steps:
                def __init__(self, base):
                    self.base, self.n = base, 0

                def then(self, ins):
                    self.n += 1
                    ins.then_inc(step, 1)
                    dve.wait_ge(step, self.base + self.n)

            def spread(col, n=NT):
                return col.rearrange("p (t o) -> p t o", o=1).broadcast_to([P, n, D])

            def rsqrt(steps, y, v, t):
                steps.then(nc.vector.tensor_scalar(y.bitcast(I32), v.bitcast(I32), -0.5, RSQRT_GUESS,
                                                   ALU.mult, ALU.add))
                for _ in range(3):
                    steps.then(nc.vector.tensor_tensor(t, y, y, ALU.mult))
                    steps.then(nc.vector.scalar_tensor_tensor(out=t, in0=t, scalar=-0.5, in1=v,
                                                              op0=ALU.mult, op1=ALU.mult))
                    steps.then(nc.vector.scalar_tensor_tensor(out=y, in0=t, scalar=1.5, in1=y,
                                                              op0=ALU.add, op1=ALU.mult))

            def ends(dst, half, dones):
                n = (half.stop - half.start) // len(dones)
                for c, done in enumerate(dones):
                    lo = half.start + c * n
                    yield slice(lo, lo + n), dst[c], done

            def norm(steps, src, dst, half, dones, scale=None):
                total, mean, var, t, y = (small[:, c, half] for c in range(5))
                c1, c2 = cen[:, half, :], cen2[:, half, :]
                n = half.stop - half.start
                steps.then(nc.vector.reduce_sum(total, src, AX))
                steps.then(nc.vector.tensor_scalar(mean, total, 1.0 / D, None, ALU.mult))
                steps.then(nc.vector.tensor_tensor(c1, src, spread(mean, n), ALU.subtract))
                steps.then(nc.vector.tensor_tensor(c2, c1, c1, ALU.mult))
                steps.then(nc.vector.reduce_sum(total, c2, AX))
                steps.then(nc.vector.tensor_scalar(var, total, 1.0 / D, EPS, ALU.mult, ALU.add))
                rsqrt(steps, y, var, t)
                if scale is not None:
                    steps.then(nc.vector.tensor_tensor(y, y, scale, ALU.mult))
                for part, to, done in ends(dst, half, dones):
                    y = small[:, 4, part]
                    nc.vector.scalar_tensor_tensor(
                        out=to, in0=cen[:, part, :], scalar=0.0, in1=spread(y, n // len(dones)),
                        op0=ALU.max, op1=ALU.mult).then_inc(done, 1)

            KEPT_BEFORE = {2: 0, 3: T, 6: 2 * T, 7: 3 * T}
            POST_STEPS = {1: 0, 2: 34, 3: 42, 4: 0, 5: 0, 6: 38, 7: 1}
            steps_used = [0]

            def post(k, s):
                i = strip_of(k, s)
                strip_tiles = bass.ds(i * NT, NT)
                x_strip = resid[:, strip_tiles, :]
                z = post_ps[:, :].rearrange("p (t d) -> p t d", d=D)
                steps = Steps(steps_used[0] + POST_STEPS[k] * s)
                computed(dve, x_strip, dinv[:, strip_tiles], result[:, strip_tiles, :])
                for h in range(2):
                    tiles = bass.ds(i * NT + h * NT // 2, NT // 2)
                    computed(dve, resid[:, tiles, :], vecs[:, tiles, k % 2, :],
                             vecs[:, tiles, 0, :], dinv[:, tiles])
                if k != 2:
                    dve.wait_ge(post_done, strips_before(k, s) + 1)
                dve.wait_ge(vec_ready, strips_before(k + 1, s))
                if k in KEPT_BEFORE:
                    dve.wait_ge(resid_kept, STARTED + KEPT_BEFORE[k] + (s if k < SWEEPS else 0))
                if k == 7:
                    steps.then(nc.vector.tensor_tensor(cen[:, :, :], z, spread(dinv[:, strip_tiles]),
                                                       ALU.mult))
                    nc.vector.tensor_tensor(result[:, strip_tiles, :], x_strip, cen[:, :, :],
                                            ALU.add).then_inc(vec_ready, 1)
                else:
                    if is_last(s):
                        update(k, s, slice(0, NT), steps, z, (vec_begun, vec_ready))
                    else:
                        update(k, s, slice(0, NT // 2), steps, z, (vec_begun,))
                        update(k, s, slice(NT // 2, NT), steps, z, (vec_ready,))
                if k in (2, 3, 6):
                    nc.vector.tensor_copy(x_strip, new_x[:, :, :]).then_inc(resid_kept, 1)
                if is_last(s):
                    steps_used[0] += POST_STEPS[k] * (T - 1) + steps.n
                else:
                    assert steps.n == POST_STEPS[k], (k, steps.n)

            def update(k, s, half, steps, z, dones):
                n = half.stop - half.start
                first = strip_of(k, s) * NT
                tiles = bass.ds(first + half.start, n)
                x_i, h_i = resid[:, tiles, :], vecs[:, tiles, 0, :]
                m = n // len(dones)
                v_next = [vecs[:, bass.ds(first + half.start + c * m, m), k % 2, :]
                          for c in range(len(dones))]
                new, c1, c2 = new_x[:, half, :], cen[:, half, :], cen2[:, half, :]
                z_all, z = z, z[:, half]
                if k == 2:
                    dve.wait_ge(tanh_ready, 2 * s + half.stop // (NT // 2))
                    steps.then(nc.vector.tensor_tensor(new, new, x_i, ALU.add))
                    norm(steps, new, v_next, half, dones)
                elif k == 3:
                    dot = small[:, 5, half]
                    steps.then(nc.vector.tensor_tensor(c1, z, h_i, ALU.mult))
                    steps.then(nc.vector.reduce_sum(dot, c1, AX))
                    steps.then(nc.vector.tensor_scalar(dot, dot, -R_CONST, F_CONST, ALU.mult,
                                                       ALU.add))
                    steps.then(nc.vector.scalar_tensor_tensor(out=c2, in0=h_i, scalar=-B_CONST,
                                                              in1=spread(dot, n), op0=ALU.mult,
                                                              op1=ALU.add))
                    steps.then(nc.vector.tensor_tensor(new, x_i, c2, ALU.add))
                    norm(steps, new, v_next, half, dones)
                elif k in (4, 5):
                    for part, to, done in ends(v_next, half, dones):
                        nc.vector.tensor_tensor(
                            to, z_all[:, part], bias_sb[:, k - 4:k - 3, :].broadcast_to([P, m, D]),
                            ALU.add).then_inc(done, 1)
                elif k == 6:
                    b = bias_sb[:, 2:3, :].broadcast_to([P, n, D])
                    steps.then(nc.vector.tensor_tensor(c1, z, b, ALU.add))
                    steps.then(nc.vector.tensor_tensor(new, x_i, c1, ALU.add))
                    norm(steps, new, v_next, half, dones, scale=dinv[:, tiles])

            def add_alone(k, s):
                fin, _, cols = parts(k, s)
                n = s if k == 1 else T + s - 1
                own, moved = slice(0, BANK), slice(BANK, SW)
                if k == 1:
                    to = [sum_sb[fin, own], sum_sb[fin, moved]]
                    dve.wait_ge(sum_begun, s + 1)
                else:
                    i = strip_of(k, s)
                    to = [partial[fin, bass.ds(i * SW + c * BANK, BANK)] for c in range(NI)]
                    computed(dve, *to)
                    dve.wait_ge(post_done, strips_before(k, s))
                dve.wait_ge(alone_done, n + 1)
                nc.vector.tensor_tensor(sum_sb[fin, own], alone_ps[fin, :], to[0],
                                        ALU.add).then_inc(alone_split, 1)
                after(dve, sum_ready, strips_before(k, s))
                nc.vector.tensor_copy(alone_moved[fin, :], alone_ps[D:P, :]).then_inc(alone_split, 1)
                dve.wait_ge(alone_split, 2 * n + 2)
                nc.vector.tensor_tensor(sum_sb[fin, moved], alone_moved[fin, :], to[1],
                                        ALU.add).then_inc(sum_ready, 1)

            def fold(k, d):
                g = k % 2
                half, other = slice(g * D, (g + 1) * D), slice((1 - g) * D, (2 - g) * D)
                i = strip_of(k, d)
                own, moved = (partial[half, bass.ds(i * SW + c * BANK, BANK)] for c in (g, 1 - g))
                n = folds_before(k, d)
                computed(dve, own, moved, n)
                dve.wait_ge(partial_kept, n + 1)
                dve.wait_ge(next_done, n + 1)
                nc.vector.tensor_tensor(own, next_ps[half, :], own, ALU.add).then_inc(next_split, 1)
                dve.wait_ge(folded, STARTED + n)
                nc.vector.tensor_copy(next_moved[half, :], next_ps[other, :]).then_inc(next_split, 1)
                dve.wait_ge(next_split, 2 * n + 2)
                nc.vector.tensor_tensor(moved, next_moved[half, :], moved, ALU.add).then_inc(folded, 1)

            def parts(k, s):
                fin, beg = D * ((k - 1) % 2), D * (k % 2)
                cols = bass.ds(strip_of(k, s) * SW, SW)
                fin, beg = slice(fin, fin + D), slice(beg, beg + D)
                computed(dve, partial[fin, cols], partial[beg, cols])
                return fin, beg, cols

            def copy_shared(k, s):
                fin, beg, cols = parts(k, s)
                banks = shared_ps[:, :, :].rearrange("p b i -> p (b i)")
                if k > 1:
                    apart(dve)
                after(dve, post_done, strips_before(k, s))
                if is_first(s):
                    if k == 1:
                        nc.vector.memset(sum_sb[fin, :], 0.0).then_inc(sum_begun, 1)
                    else:
                        nc.vector.tensor_copy(sum_sb[fin, :], partial[fin, cols]).then_inc(
                            sum_ready, 1)
                    if k < SWEEPS:
                        nc.vector.memset(partial[beg, cols], 0.0).then_inc(partial_kept, 1)
                    return
                dve.wait_ge(shared_done, (T - 1) * (k - 1) + s)
                nc.vector.tensor_tensor(sum_sb[fin, :], banks[fin], partial[fin, cols],
                                        ALU.add).then_inc(sum_ready, 1)
                nc.vector.tensor_copy(partial[beg, cols], banks[beg]).then_inc(partial_kept, 1)

            def add_rows(s, src, landed, landings, row, units=range(NQ)):
                computed(dve, 2 * (s + 1), landings)
                for q in units:
                    if q == 0:
                        dve.wait_ge(rows_cleared, 2 * (s + 1))
                    dve.wait_ge(landed[q], landings)
                    after(dve, rows_added, NQ * row + q)
                    nc.vector.tensor_tensor(row_sums[:, :, :], row_sums[:, :, :], src[:, q],
                                            ALU.add).then_inc(rows_added, 1)

            def fold_rows(s):
                dve.wait_ge(rows_added, NQ * T * (s + 1))
                nc.vector.tensor_tensor(row_sums[:, 0], row_sums[:, 0], row_sums[:, 1],
                                        ALU.add).then_inc(rows_folded, 1)

            def copy_degrees(s):
                dve.wait_ge(deg_done, s + 1)
                nc.vector.tensor_copy(degree[:, bass.ds(s * NT, NT)], deg_ps[:, 0:NT]).then_inc(
                    deg_copied, 1)

            def inverse_roots():
                steps = Steps(steps_used[0])
                deg, floor, y, t = (dtmp[:, c, :] for c in range(4))
                dve.wait_ge(deg_copied, STARTED + T)
                steps.then(nc.vector.tensor_scalar(deg, degree[:, :], 1.0, None, ALU.add))
                steps.then(nc.vector.tensor_scalar(floor, deg, TINY, None, ALU.max))
                rsqrt(steps, y, floor, t)
                steps.then(nc.vector.scalar_tensor_tensor(out=dinv[:, :], in0=deg, scalar=0.0, in1=y,
                                                          op0=ALU.is_gt, op1=ALU.mult))
                steps_used[0] += steps.n

            def first_norm():
                tiles = slice(FIRST_USED[0] * NT, (FIRST_USED[0] + 1) * NT)
                dve.wait_ge(x_loaded[0], 16)
                steps = Steps(steps_used[0])
                norm(steps, resid[:, tiles, :], [vecs[:, tiles, 0, :]], slice(0, NT), (vec_ready,))
                steps_used[0] += steps.n

            def mean(n):
                tiles = slice(FIRST_USED[n] * NT, (FIRST_USED[n] + 1) * NT)
                dve.wait_ge(x_summed, n)
                nc.vector.tensor_scalar(neg_mean[:, tiles], x_sum[:, tiles], -1.0 / D, None,
                                        ALU.mult).then_inc(mean_ready, 1)

            def scale_and_shift(n):
                tiles = slice(FIRST_USED[n] * NT, (FIRST_USED[n] + 1) * NT)
                steps = Steps(steps_used[0])
                var, t = small[:, 2, :], small[:, 3, :]
                dve.wait_ge(mean_ready, n)
                dve.wait_ge(x_squared, n)
                steps.then(nc.vector.tensor_scalar(var, x_dev[:, tiles], 1.0 / D, EPS, ALU.mult,
                                                   ALU.add))
                rsqrt(steps, x_scale[:, tiles], var, t)
                nc.vector.tensor_tensor(x_shift[:, tiles], x_scale[:, tiles], neg_mean[:, tiles],
                                        ALU.mult).then_inc(scale_ready, 1)
                steps_used[0] += steps.n

            def strip(k, s, early=False):
                if k == 1:
                    if not is_first(s):
                        copy_degrees(s - 1)
                    if is_first(s):
                        for a in range(T - 1):
                            add_rows(s, right, right_landed, 16 * (a + 1), a, units=(0,))
                            scale_and_shift(a + 1)
                            if a + 2 < T:
                                mean(a + 2)
                            add_rows(s, right, right_landed, 16 * (a + 1), a, units=range(1, NQ))
                        add_rows(s, diag, diag_landed, 16, T - 1)
                        fold_rows(s)
                        add_alone(k, s)
                        return
                    else:
                        sweep_one(dve, s, early,
                                  lambda _, n, row, *__: add_rows(s, right, right_landed,
                                                                  16 * (n + 1), row),
                                  lambda _, n, row, *__: add_rows(s, tri, tri_landed,
                                                                  16 * (n + 1), row),
                                  lambda _: None,
                                  lambda _, row: add_rows(s, diag, diag_landed, 16 * (s + 1), row))
                        fold_rows(s)
                        fold(k, s - 1)
                    add_alone(k, s)
                    return
                if not is_first(s):
                    post(k, s - 1)
                    if k < SWEEPS and not (isinstance(s, int) and s == 1):
                        fold(k, s - 2)
                if is_first(s) or k < SWEEPS:
                    copy_shared(k, s)
                else:
                    add_alone(k, s)
                if k == 2 and is_first(s):
                    copy_degrees(T - 1)
                    inverse_roots()

            copy_shared(1, 0)
            first_norm()
            mean(1)
            for k in range(1, SWEEPS + 1):
                if k == 2:
                    dve.wait_ge(w_loaded, 16 * 5)
                if k > 1:
                    dve.wait_ge(folded, STARTED + T * (k - 1))
                over_strips(dve, k, strip)
                if k == 1:
                    fold(k, T - 1)
                    continue
                post(k, T - 1)
                if k < SWEEPS:
                    fold(k, T - 2)
                    fold(k, T - 1)


def kernel(x, adj, L0_gnn_W, L1_gnn_t, L2_gnn_W0, L2_gnn_b0, L2_gnn_W1, L2_gnn_b1, L2_gnn_W2,
           L2_gnn_b2, L3_gnn_W):
    import numpy as np
    import concourse.bacc as bacc
    from concourse import mybir as mb
    from concourse.bass_utils import run_bass_kernel_spmd

    n = x.shape[0]
    t = n // SW
    a = {}
    a["x_rows"] = np.ascontiguousarray(np.asarray(x).reshape(n // P, P, D).transpose(1, 0, 2))
    a["adj_units"] = np.ascontiguousarray(
        np.asarray(adj).reshape(t, SW, t, NQ, 2, P).transpose(0, 2, 3, 5, 4, 1)).reshape(
            t * t * NQ, P, 2 * SW)
    w0 = np.asarray(L0_gnn_W)
    eye = np.eye(P, dtype=np.float32)
    a["w_right"] = np.stack([w0[0, :D], w0[1, :D], eye[:D, :D], np.asarray(L2_gnn_W0).T,
                             np.asarray(L2_gnn_W1).T, np.asarray(L2_gnn_W2).T, np.asarray(L3_gnn_W)])
    w3 = np.asarray(L3_gnn_W)
    a["w_concat"] = np.stack([w0[0], np.concatenate([w0[1, D:], w0[1, :D]]),
                              np.concatenate([w3, w3])])
    a["bias_rows"] = np.ascontiguousarray(np.broadcast_to(
        np.stack([np.asarray(b) for b in (L2_gnn_b0, L2_gnn_b1, L2_gnn_b2)]), (P, 3, D)))
    a["eye"] = eye
    nc = bacc.Bacc("TRN2", target_bir_lowering=False, num_devices=1)
    aps = [nc.dram_tensor(name, v.shape, mb.dt.float32, kind="ExternalInput").ap()
           for name, v in a.items()]
    out = nc.dram_tensor("out_rows", a["x_rows"].shape, mb.dt.float32, kind="ExternalOutput").ap()
    graph_layers(nc, *aps, out)
    r = run_bass_kernel_spmd(nc, [a], core_ids=[0])
    rows = r.results[0]["out_rows"]
    return np.ascontiguousarray(rows.transpose(1, 0, 2)).reshape(n, D)
```
